# Optimizing a Trainium2 kernel written in Bass

```python
import numpy as np
import jax
import jax.numpy as jnp

def _softmax(x, axis=-1):
    return jax.nn.softmax(x, axis=axis)

def _gelu(x):
    return jax.nn.gelu(x, approximate=True)

def _silu(x):
    return jax.nn.silu(x)

def _sigmoid(x):
    return jax.nn.sigmoid(x)

def _layernorm(x, axis=-1, eps=1e-05):
    m = jnp.mean(x, axis=axis, keepdims=True)
    v = jnp.var(x, axis=axis, keepdims=True)
    return (x - m) / jnp.sqrt(v + eps)

def _scatter_add(tgt, idx, src, axis=0):
    return tgt.at[idx].add(src)

def _segment_sum(src, seg, n):
    return jax.ops.segment_sum(src, seg, n)
kernel_name = 'mk_dlrm_tower_d1_rec_r8_32f0d0'

def setup_inputs(seed: int=0):
    np.random.seed(seed)
    _w = jnp.asarray

    def _rec_inputs():
        import jax
        import jax.numpy as jnp
        _tk = jax.random.key(seed)
        dense_ctx = jax.random.normal(jax.random.fold_in(_tk, 190), (512, 16), jnp.float32)
        ids = jnp.stack([jax.random.randint(jax.random.fold_in(_tk, 200 + f), (512,), 0, v, jnp.int32) for f, v in enumerate([1250, 1250, 1000, 1000, 1000, 12500, 12500, 1250, 12500, 1000, 1000, 125000, 125000, 1250, 12500, 12500, 12500, 1000, 125000, 125000, 125000, 12500, 12500, 1000, 125000, 12500])], axis=1)
        tbl_0 = 0.05 * jax.random.normal(jax.random.fold_in(_tk, 500 + 0), (1250, 32), jnp.float32)
        tbl_1 = 0.05 * jax.random.normal(jax.random.fold_in(_tk, 500 + 1), (1250, 32), jnp.float32)
        tbl_2 = 0.05 * jax.random.normal(jax.random.fold_in(_tk, 500 + 2), (1000, 32), jnp.float32)
        tbl_3 = 0.05 * jax.random.normal(jax.random.fold_in(_tk, 500 + 3), (1000, 32), jnp.float32)
        tbl_4 = 0.05 * jax.random.normal(jax.random.fold_in(_tk, 500 + 4), (1000, 32), jnp.float32)
        tbl_5 = 0.05 * jax.random.normal(jax.random.fold_in(_tk, 500 + 5), (12500, 32), jnp.float32)
        tbl_6 = 0.05 * jax.random.normal(jax.random.fold_in(_tk, 500 + 6), (12500, 32), jnp.float32)
        tbl_7 = 0.05 * jax.random.normal(jax.random.fold_in(_tk, 500 + 7), (1250, 32), jnp.float32)
        tbl_8 = 0.05 * jax.random.normal(jax.random.fold_in(_tk, 500 + 8), (12500, 32), jnp.float32)
        tbl_9 = 0.05 * jax.random.normal(jax.random.fold_in(_tk, 500 + 9), (1000, 32), jnp.float32)
        tbl_10 = 0.05 * jax.random.normal(jax.random.fold_in(_tk, 500 + 10), (1000, 32), jnp.float32)
        tbl_11 = 0.05 * jax.random.normal(jax.random.fold_in(_tk, 500 + 11), (125000, 32), jnp.float32)
        tbl_12 = 0.05 * jax.random.normal(jax.random.fold_in(_tk, 500 + 12), (125000, 32), jnp.float32)
        tbl_13 = 0.05 * jax.random.normal(jax.random.fold_in(_tk, 500 + 13), (1250, 32), jnp.float32)
        tbl_14 = 0.05 * jax.random.normal(jax.random.fold_in(_tk, 500 + 14), (12500, 32), jnp.float32)
        tbl_15 = 0.05 * jax.random.normal(jax.random.fold_in(_tk, 500 + 15), (12500, 32), jnp.float32)
        tbl_16 = 0.05 * jax.random.normal(jax.random.fold_in(_tk, 500 + 16), (12500, 32), jnp.float32)
        tbl_17 = 0.05 * jax.random.normal(jax.random.fold_in(_tk, 500 + 17), (1000, 32), jnp.float32)
        tbl_18 = 0.05 * jax.random.normal(jax.random.fold_in(_tk, 500 + 18), (125000, 32), jnp.float32)
        tbl_19 = 0.05 * jax.random.normal(jax.random.fold_in(_tk, 500 + 19), (125000, 32), jnp.float32)
        tbl_20 = 0.05 * jax.random.normal(jax.random.fold_in(_tk, 500 + 20), (125000, 32), jnp.float32)
        tbl_21 = 0.05 * jax.random.normal(jax.random.fold_in(_tk, 500 + 21), (12500, 32), jnp.float32)
        tbl_22 = 0.05 * jax.random.normal(jax.random.fold_in(_tk, 500 + 22), (12500, 32), jnp.float32)
        tbl_23 = 0.05 * jax.random.normal(jax.random.fold_in(_tk, 500 + 23), (1000, 32), jnp.float32)
        tbl_24 = 0.05 * jax.random.normal(jax.random.fold_in(_tk, 500 + 24), (125000, 32), jnp.float32)
        tbl_25 = 0.05 * jax.random.normal(jax.random.fold_in(_tk, 500 + 25), (12500, 32), jnp.float32)
        _rk = jax.random.fold_in(_tk, 7)
        W_top1 = 0.0606339 * jax.random.normal(jax.random.fold_in(_tk, 801), (272, 512), jnp.float32)
        W_top2 = 0.0441942 * jax.random.normal(jax.random.fold_in(_tk, 802), (512, 256), jnp.float32)
        W_top3 = 0.0625 * jax.random.normal(jax.random.fold_in(_tk, 803), (256, 1), jnp.float32)
        b_top1 = jnp.zeros((512,), jnp.float32)
        b_top2 = jnp.zeros((256,), jnp.float32)
        return (dense_ctx, ids, tbl_0, tbl_1, tbl_2, tbl_3, tbl_4, tbl_5, tbl_6, tbl_7, tbl_8, tbl_9, tbl_10, tbl_11, tbl_12, tbl_13, tbl_14, tbl_15, tbl_16, tbl_17, tbl_18, tbl_19, tbl_20, tbl_21, tbl_22, tbl_23, tbl_24, tbl_25, W_top1, b_top1, W_top2, b_top2, W_top3)
    dense_ctx, ids, tbl_0, tbl_1, tbl_2, tbl_3, tbl_4, tbl_5, tbl_6, tbl_7, tbl_8, tbl_9, tbl_10, tbl_11, tbl_12, tbl_13, tbl_14, tbl_15, tbl_16, tbl_17, tbl_18, tbl_19, tbl_20, tbl_21, tbl_22, tbl_23, tbl_24, tbl_25, W_top1, b_top1, W_top2, b_top2, W_top3 = _rec_inputs()

    def _L0_rec_setup():
        import jax, jax.numpy as jnp
        import numpy as np
        M_FIELDS = 26
        H1 = 128
        H2 = 128
        BATCH = 256
        EMB_K = 32

        def _cin_layer(x_prev, x0, W, b):
            return jnp.einsum('bik,bjk,hij->bhk', x_prev, x0, W) + b[None, :, None]
        key = jax.random.key(seed)
        k0, k1, k2, k3, k4 = jax.random.split(key, 5)
        inputs = jax.random.normal(k0, (BATCH, M_FIELDS, EMB_K), dtype=jnp.float32)
        W1 = jax.random.normal(k1, (H1, M_FIELDS, M_FIELDS), dtype=jnp.float32) * 0.05
        b1 = jax.random.normal(k2, (H1,), dtype=jnp.float32) * 0.05
        W2 = jax.random.normal(k3, (H2, H1, M_FIELDS), dtype=jnp.float32) * 0.05
        b2 = jax.random.normal(k4, (H2,), dtype=jnp.float32) * 0.05
        return {'inputs': inputs, 'W1': W1, 'b1': b1, 'W2': W2, 'b2': b2}
    _L0_rec_all = _L0_rec_setup()
    _L0_rec_in = {k: v for k, v in _L0_rec_all.items() if k in ('W1', 'b1', 'W2', 'b2')}
    del _L0_rec_all
    return {'dense_ctx': dense_ctx, 'ids': ids, 'tbl_0': tbl_0, 'tbl_1': tbl_1, 'tbl_2': tbl_2, 'tbl_3': tbl_3, 'tbl_4': tbl_4, 'tbl_5': tbl_5, 'tbl_6': tbl_6, 'tbl_7': tbl_7, 'tbl_8': tbl_8, 'tbl_9': tbl_9, 'tbl_10': tbl_10, 'tbl_11': tbl_11, 'tbl_12': tbl_12, 'tbl_13': tbl_13, 'tbl_14': tbl_14, 'tbl_15': tbl_15, 'tbl_16': tbl_16, 'tbl_17': tbl_17, 'tbl_18': tbl_18, 'tbl_19': tbl_19, 'tbl_20': tbl_20, 'tbl_21': tbl_21, 'tbl_22': tbl_22, 'tbl_23': tbl_23, 'tbl_24': tbl_24, 'tbl_25': tbl_25, 'W_top1': W_top1, 'b_top1': b_top1, 'W_top2': W_top2, 'b_top2': b_top2, 'W_top3': W_top3, 'L0_rec_W1': _L0_rec_in['W1'], 'L0_rec_b1': _L0_rec_in['b1'], 'L0_rec_W2': _L0_rec_in['W2'], 'L0_rec_b2': _L0_rec_in['b2']}

def reference(dense_ctx, ids, tbl_0, tbl_1, tbl_2, tbl_3, tbl_4, tbl_5, tbl_6, tbl_7, tbl_8, tbl_9, tbl_10, tbl_11, tbl_12, tbl_13, tbl_14, tbl_15, tbl_16, tbl_17, tbl_18, tbl_19, tbl_20, tbl_21, tbl_22, tbl_23, tbl_24, tbl_25, W_top1, b_top1, W_top2, b_top2, W_top3, L0_rec_W1, L0_rec_b1, L0_rec_W2, L0_rec_b2):
    import jax
    import jax.numpy as jnp

    def _L0_rec_ref(inputs, W1, b1, W2, b2):
        import jax, jax.numpy as jnp
        import numpy as np
        M_FIELDS = 26
        H1 = 128
        H2 = 128
        BATCH = 256
        EMB_K = 32

        def _cin_layer(x_prev, x0, W, b):
            return jnp.einsum('bik,bjk,hij->bhk', x_prev, x0, W) + b[None, :, None]
        x1 = _cin_layer(inputs, inputs, W1, b1)
        x2 = _cin_layer(x1, inputs, W2, b2)
        res = jnp.concatenate([x1, x2], axis=1)
        return jnp.sum(res, axis=-1)
    e = jnp.stack([tbl_0[ids[:, 0]], tbl_1[ids[:, 1]], tbl_2[ids[:, 2]], tbl_3[ids[:, 3]], tbl_4[ids[:, 4]], tbl_5[ids[:, 5]], tbl_6[ids[:, 6]], tbl_7[ids[:, 7]], tbl_8[ids[:, 8]], tbl_9[ids[:, 9]], tbl_10[ids[:, 10]], tbl_11[ids[:, 11]], tbl_12[ids[:, 12]], tbl_13[ids[:, 13]], tbl_14[ids[:, 14]], tbl_15[ids[:, 15]], tbl_16[ids[:, 16]], tbl_17[ids[:, 17]], tbl_18[ids[:, 18]], tbl_19[ids[:, 19]], tbl_20[ids[:, 20]], tbl_21[ids[:, 21]], tbl_22[ids[:, 22]], tbl_23[ids[:, 23]], tbl_24[ids[:, 24]], tbl_25[ids[:, 25]]], axis=1)
    z = _L0_rec_ref(e, L0_rec_W1, L0_rec_b1, L0_rec_W2, L0_rec_b2)
    z = z.reshape(z.shape[0], -1)
    h = jnp.concatenate([z, dense_ctx], axis=1)
    h = jnp.maximum(h @ W_top1 + b_top1, 0.0)
    h = jnp.maximum(h @ W_top2 + b_top2, 0.0)
    y = h @ W_top3
    return y

_drawn_inputs = setup_inputs


def setup_inputs(seed=0):
    import zlib

    import numpy as np

    out = dict(_drawn_inputs(seed))
    spreads = {'b_top1': (0.0, 0.8), 'b_top2': (0.0, 0.8)}
    factors = {'tbl_0': 8.0,
     'tbl_1': 8.0,
     'tbl_2': 8.0,
     'tbl_3': 8.0,
     'tbl_4': 8.0,
     'tbl_5': 8.0,
     'tbl_6': 8.0,
     'tbl_7': 8.0,
     'tbl_8': 8.0,
     'tbl_9': 8.0,
     'tbl_10': 8.0,
     'tbl_11': 8.0,
     'tbl_12': 8.0,
     'tbl_13': 8.0,
     'tbl_14': 8.0,
     'tbl_15': 8.0,
     'tbl_16': 8.0,
     'tbl_17': 8.0,
     'tbl_18': 8.0,
     'tbl_19': 8.0,
     'tbl_20': 8.0,
     'tbl_21': 7.526,
     'tbl_22': 8.0,
     'tbl_23': 8.0,
     'tbl_24': 8.0,
     'tbl_25': 8.0,
     'L0_rec_W1': 8.0,
     'L0_rec_W2': 3.983,
     'dense_ctx': 6.003}
    for name, (base, spread) in spreads.items():
        noise = np.random.default_rng([zlib.crc32(name.encode()), seed]).standard_normal(out[name].shape)
        drawn = base * np.exp(spread * noise) if base else spread * noise
        out[name] = jnp.asarray(drawn.astype(out[name].dtype))
    for name, factor in factors.items():
        out[name] = (out[name] * factor).astype(out[name].dtype)
    return out
```

```python
from contextlib import ExitStack

import concourse.bass as bass
from concourse import mybir

F32 = mybir.dt.float32
I32 = mybir.dt.int32
ALU = mybir.AluOpType
ACT = mybir.ActivationFunctionType

P = 128
QUARTERS = 4
ROWS = P // QUARTERS


def tri(j):
    return j * (j + 1) // 2


def chunks_of_pairs(fields):
    cuts, j0, room = [], 0, P - 1
    for j in range(fields + 1):
        if j == fields or tri(j + 1) - tri(j0) > room:
            cuts.append((j0, j))
            j0, room = j, P
    return cuts


def dlrm_tower(nc, dense, ids, tables, W_top1, b_top1, W_top2, b_top2, W_top3, W1, b1, W2, b2, out):
    BATCH, ND = dense.shape
    NF = ids.shape[1]
    K = tables[0].shape[1]
    H = W1.shape[0]
    H1, H2 = W_top2.shape
    BLOCKS = BATCH // P
    assert H == P and K == P // QUARTERS and BATCH % P == 0 and H1 % P == 0 and H2 % P == 0
    M1, M2 = H1 // P, H2 // P
    HALF = NF // 2

    CH = chunks_of_pairs(NF)
    assert len(CH) == 3
    NCH = len(CH)
    PAIRS = [tri(b) - tri(a) + (c == 0) for c, (a, b) in enumerate(CH)]
    CONST = PAIRS[0] - 1
    LS = [NF + 1 - a for a, _ in CH]
    LOFF = [sum(LS[:c]) for c in range(NCH)]
    WIDE = [n * QUARTERS for n in LS]
    PER = [4, 8, 8]
    assert all(n * w <= 512 for n, w in zip(PER, WIDE))
    GROUPS = [ROWS // n for n in PER]
    GOFF = [sum(GROUPS[:c]) for c in range(NCH)]
    NG = sum(GROUPS)
    RING = 4
    PARTS = [0, NF // 3, 2 * NF // 3, NF]
    CUTS = [0, HALF, NF - 3, NF]

    LOW = HALF * HALF
    FW = LOW + (NF - HALF) * NF + 1

    def pos(a, b):
        return a * HALF + b if a < HALF else LOW + (a - HALF) * NF + b

    with ExitStack() as ctx:
        def sb(name, shape, dt=F32):
            return ctx.enter_context(nc.sbuf_tensor(name, shape, dt))

        def bank(name):
            return ctx.enter_context(nc.psum_tensor(name, [P, 512], F32))

        def sem(name):
            return ctx.enter_context(nc.semaphore(name))

        idx = sb("idx", [P, BLOCKS, NF], I32)
        idx_now = sb("idx_now", [P, NF], I32)
        emb = sb("emb", [P, NF, K])
        embT = sb("embT", [P, ROWS, NF])
        diag = sb("diag", [P, ROWS, NF + 1, QUARTERS])
        pairs = [sb(f"pairs{c}", [P, ROWS, PAIRS[c]]) for c in range(NCH)]
        T = sb("T", [P, sum(LS), P])
        w1_nat = sb("w1_nat", [P, NF, NF])
        w1f = sb("w1f", [P, FW])
        F = sb("F", [P, NF, FW])
        room_a = sb("room_a", [P, sum(LS) * P])
        w2_nat = room_a[:, 0:H * NF].rearrange("p (i l) -> p i l", l=NF)
        w12 = room_a[:, :].rearrange("p (l h) -> p l h", h=P)
        TRI = sum(PAIRS[c] * LS[c] for c in range(NCH))
        room_b = sb("room_b", [P, max(TRI, NF * H)])
        w2t = room_b[:, 0:NF * H].rearrange("p (l h) -> p l h", h=H)
        toff = [sum(PAIRS[d] * LS[d] for d in range(c)) for c in range(NCH)]
        w12t = [room_b[:, toff[c]:toff[c] + PAIRS[c] * LS[c]].rearrange("p (l n) -> p l n", n=PAIRS[c])
                for c in range(NCH)]
        top1 = sb("top1", [P, 2, H1])
        top1d = sb("top1d", [ND + 1, H1])
        top2 = sb("top2", [P, M1, H2])
        top3 = sb("top3", [P, M2])
        b2_sb = sb("b2_sb", [P, 1])
        kb2 = sb("kb2", [P, 1])
        bt2 = sb("bt2", [P, M2])
        dense_nat = sb("dense_nat", [P, BLOCKS, ND + 1])
        denseT = sb("denseT", [ND + 1, BLOCKS, P])
        ident = sb("ident", [P, P])
        z = sb("z", [P, 2, P])
        h1 = sb("h1", [P, M1, P])
        h2 = sb("h2", [P, M2, P])
        y = sb("y", [1, P])

        ring = [bank(f"ring{n}") for n in range(RING)]
        z_ps = bank("z_ps")
        h1_ps = bank("h1_ps")
        h2_ps = bank("h2_ps")
        turn_ps = bank("turn_ps")
        y_ps = h2_ps[0:1, M2 * P:(M2 + 1) * P]

        s_ids = sem("s_ids")
        s_w1 = sem("s_w1")
        s_w2 = sem("s_w2")
        s_dense = sem("s_dense")
        s_top = sem("s_top")
        s_ident0 = sem("s_ident0")
        s_ident = sem("s_ident")
        s_idx = sem("s_idx")
        s_emb = [sem(f"s_emb{f}") for f in range(NF)]
        s_room = sem("s_room")
        s_set = sem("s_set")
        s_w1f0 = sem("s_w1f0")
        s_w1f = sem("s_w1f")
        s_turned = sem("s_turned")
        s_pairs = sem("s_pairs")
        s_fold = sem("s_fold")
        s_w12t = sem("s_w12t")
        s_kb2 = sem("s_kb2")
        s_diag = sem("s_diag")
        s_dT_ps = sem("s_dT_ps")
        s_dT = sem("s_dT")
        s_w2t_ps = sem("s_w2t_ps")
        s_w2t = sem("s_w2t")
        s_F_ps = sem("s_F_ps")
        s_F = sem("s_F")
        s_w12_ps = sem("s_w12_ps")
        s_w12 = sem("s_w12")
        s_T_ps = sem("s_T_ps")
        s_T = sem("s_T")
        s_z_ps = sem("s_z_ps")
        s_z = sem("s_z")
        s_h1_ps = sem("s_h1_ps")
        s_h1 = sem("s_h1")
        s_h2_ps = sem("s_h2_ps")
        s_h2 = sem("s_h2")
        s_y_ps = sem("s_y_ps")
        s_y = sem("s_y")
        s_out = sem("s_out")

        W12_BATCHES = [(c, range(n, min(n + 4, LS[c]))) for c in range(NCH) for n in range(0, LS[c], 4)]
        W2_BATCHES = [range(n, min(n + 4, NF)) for n in range(0, NF, 4)]
        NTOP = 7

        block = ctx.enter_context(nc.Block())

        @block.sync
        def _(sp):
            sp.dma_start(idx[:, :, :], ids.rearrange("(q p) f -> p q f", p=P)).then_inc(s_ids, 16)
            sp.dma_start(w1_nat[:, :, :], W1).then_inc(s_w1, 16)
            sp.dma_start(w1f[:, FW - 1:FW], b1.rearrange("(p o) -> p o", o=1)).then_inc(s_w1, 16)
            sp.dma_start(room_a[0:P // 2, 0:H * NF], W2.rearrange("h i l -> h (i l)")[0:P // 2, :]).then_inc(s_w2, 16)
            sp.dma_start(dense_nat[:, :, 0:ND], dense.rearrange("(q p) d -> p q d", p=P)).then_inc(s_dense, 16)
            sp.dma_start(top1[:, :, :], W_top1[0:2 * P, :].rearrange("(c p) n -> p c n", p=P)).then_inc(s_top, 16)
            sp.dma_start(top1d[0:ND, :], W_top1[2 * P:2 * P + ND, :]).then_inc(s_top, 16)
            sp.dma_start(top1d[ND:ND + 1, :], b_top1.rearrange("(o n) -> o n", o=1)).then_inc(s_top, 16)
            sp.dma_start(top2[:, :, :], W_top2.rearrange("(c p) n -> p c n", p=P)).then_inc(s_top, 16)
            sp.dma_start(b2_sb[:, :], b2.rearrange("(p o) -> p o", o=1)).then_inc(s_top, 16)
            with nc.allow_non_contiguous_dma(reason="a few hundred words"):
                sp.dma_start(bt2[:, :], b_top2.rearrange("(c p) -> p c", p=P)).then_inc(s_top, 16)
                sp.dma_start(top3[:, :], W_top3.rearrange("(c p) o -> p (c o)", p=P)).then_inc(s_top, 16)
            with nc.sync.Fori(0, BLOCKS) as b:
                sp.wait_ge(s_y, b + 1)
                sp.dma_start(out[bass.ds(b * P, P), :].rearrange("p o -> o p"), y[:, :]).then_inc(s_out, 16)
            sp.wait_ge(s_out, 16 * BLOCKS)

        @block.gpsimd
        def _(pool):
            nc.gpsimd.memset(ident[:, :], 0.0).then_inc(s_ident0, 1)
            pool.wait_ge(s_ident0, 1)
            nc.gpsimd.affine_select(out=ident[:, :], in_=ident[:, :], compare_op=ALU.not_equal, fill=1.0, base=0,
                                    pattern=[[-1, P]], channel_multiplier=1).then_inc(s_ident, 1)
            pool.wait_ge(s_ids, 16)

            def gathers(b, later):
                for part in range(len(PARTS) - 1):
                    f0, f1 = PARTS[part], PARTS[part + 1]
                    if later:
                        pool.wait_ge(s_turned, b * NF - NF + f1)
                        pool.sem_inc(s_room, 1)
                    ids_now = (idx[:, bass.ds(b, 1), f0:f1].rearrange("p o f -> p (o f)") if later
                               else idx[:, b, f0:f1])
                    nc.gpsimd.tensor_copy(idx_now[:, f0:f1], ids_now).then_inc(s_idx, 1)
                    pool.wait_ge(s_idx, b * (len(PARTS) - 1) + part + 1)
                    if later:
                        pool.sem_inc(s_room, 1)
                    for f in range(f0, f1):
                        nc.gpsimd.indirect_dma_start(emb[:, f, :], None, tables[f],
                                                     bass.IndirectOffsetOnAxis(ap=idx_now[:, f:f + 1], axis=0)
                                                     ).then_inc(s_emb[f], 16)

            gathers(0, False)
            with nc.gpsimd.Fori(1, BLOCKS) as b:
                gathers(b, True)

        @block.scalar
        def _(act):
            act.dma_start(room_a[P // 2:P, 0:H * NF], W2.rearrange("h i l -> h (i l)")[P // 2:P, :]).then_inc(s_w2, 16)
            act.wait_ge(s_dT_ps, 1)
            nc.scalar.copy(denseT[:, :, :].rearrange("p b (r q) -> p b q r", q=QUARTERS),
                           h1_ps[0:ND + 1, :].rearrange("p (b q r) -> p b q r", b=BLOCKS, q=QUARTERS)).then_inc(s_dT, 1)
            for n, batch in enumerate(W2_BATCHES):
                act.wait_ge(s_w2t_ps, n + 1)
                nc.scalar.copy(w2t[:, batch[0]:batch[-1] + 1, :],
                               ring[n % 2][:, 0:len(batch) * P].rearrange("p (l h) -> p l h", h=P)).then_inc(s_w2t, 1)
            for c in range(NF):
                act.wait_ge(s_F_ps, c + 1)
                nc.scalar.copy(F[:, c, :], ring[2 + c % 2][:, 0:FW]).then_inc(s_F, 1)
            act.wait_ge(s_top, 16 * NTOP)
            nc.scalar.mul(kb2[:, :], b2_sb[:, :], float(K)).then_inc(s_kb2, 1)

            def spread(b):
                for part in range(len(CUTS) - 1):
                    f0, f1 = CUTS[part], CUTS[part + 1]
                    act.wait_ge(s_turned, NF * b + f1)
                    for q in range(QUARTERS):
                        quarter = slice(q * ROWS, (q + 1) * ROWS)
                        last = nc.scalar.copy(diag[quarter, :, f0:f1, q], embT[quarter, :, f0:f1])
                    last.then_inc(s_diag, 1)

            def keep_T(b, c):
                for g in range(GROUPS[c]):
                    n = GOFF[c] + g
                    act.wait_ge(s_T_ps, NG * b + n + 1)
                    src = ring[n % RING][0:PAIRS[c], 0:PER[c] * WIDE[c]].rearrange(
                        "p (r l q) -> p l r q", r=PER[c], q=QUARTERS)
                    dst = T[0:PAIRS[c], LOFF[c]:LOFF[c] + LS[c],
                            g * PER[c] * QUARTERS:(g + 1) * PER[c] * QUARTERS].rearrange(
                        "p l (r q) -> p l r q", q=QUARTERS)
                    nc.scalar.copy(dst, src).then_inc(s_T, 1)

            def keep_z(b):
                act.wait_ge(s_z_ps, b + 1)
                nc.scalar.copy(z[:, 0, :], z_ps[:, 0:P])
                nc.scalar.activation(z[:, 1, :], z_ps[:, P:2 * P], ACT.Identity, bias=kb2[:, 0:1]).then_inc(s_z, 1)

            def relu1(b):
                act.wait_ge(s_h1_ps, b + 1)
                nc.scalar.activation(h1[:, :, :], h1_ps[:, 0:M1 * P].rearrange("p (m n) -> p m n", n=P),
                                     ACT.Relu).then_inc(s_h1, 1)

            def relu2(b):
                act.wait_ge(s_h2_ps, b + 1)
                for m in range(M2):
                    last = nc.scalar.activation(h2[:, m, :], h2_ps[:, m * P:(m + 1) * P], ACT.Relu, bias=bt2[:, m:m + 1])
                last.then_inc(s_h2, 1)

            def keep_y(b, later=True):
                act.wait_ge(s_y_ps, b + 1)
                if later:
                    act.wait_ge(s_out, 16 * b)
                nc.scalar.copy(y[:, :].rearrange("p (q r) -> p r q", q=QUARTERS),
                               y_ps.rearrange("p (r q) -> p r q", q=QUARTERS)).then_inc(s_y, 1)

            act.wait_ge(s_set, 1)
            spread(0)
            for c in range(NCH):
                keep_T(0, c)
            for n, (c, ls) in enumerate(W12_BATCHES):
                act.wait_ge(s_w12_ps, n + 1)
                nc.scalar.copy(w12[0:PAIRS[c], LOFF[c] + ls[0]:LOFF[c] + ls[-1] + 1, :],
                               (turn_ps if n % 2 else h1_ps)[0:PAIRS[c], 0:len(ls) * P].rearrange(
                                   "p (l h) -> p l h", h=P)).then_inc(s_w12, 1)
            act.wait_ge(s_kb2, 1)
            keep_z(0)
            spread(1)
            keep_T(1, 0)
            relu1(0)
            keep_T(1, 1)
            relu2(0)
            keep_T(1, 2)
            keep_y(0, False)
            with nc.scalar.Fori(1, BLOCKS - 1) as b:
                keep_z(b)
                spread(b + 1)
                keep_T(b + 1, 0)
                relu1(b)
                keep_T(b + 1, 1)
                relu2(b)
                keep_T(b + 1, 2)
                keep_y(b)
            keep_z(BLOCKS - 1)
            relu1(BLOCKS - 1)
            relu2(BLOCKS - 1)
            keep_y(BLOCKS - 1)

        @block.vector
        def _(dve):
            nc.vector.memset(diag[:, :, :, :], 0.0)
            nc.vector.memset(dense_nat[:, :, ND:ND + 1], 1.0)
            nc.vector.memset(pairs[0][:, :, CONST:CONST + 1], 1.0).then_inc(s_set, 1)
            dve.wait_ge(s_set, 1)
            for q in range(QUARTERS):
                last = nc.vector.memset(diag[q * ROWS:(q + 1) * ROWS, :, NF, q], 1.0)
            last.then_inc(s_set, 1)

            dve.wait_ge(s_w1, 32)
            low = w1f[:, 0:LOW].rearrange("p (a b) -> p a b", b=HALF)
            high = w1f[:, LOW:FW - 1].rearrange("p (a b) -> p a b", b=NF)
            turned = w1_nat[:, :, :].rearrange("p a b -> p b a")
            nc.vector.tensor_tensor(low, w1_nat[:, 0:HALF, 0:HALF], turned[:, 0:HALF, 0:HALF], ALU.add)
            nc.vector.tensor_tensor(high, w1_nat[:, HALF:NF, :], turned[:, HALF:NF, :], ALU.add).then_inc(s_w1f0, 1)
            flat = w1_nat[:, :, :].rearrange("p a b -> p (a b)")
            dve.wait_ge(s_w1f0, 1)
            nc.vector.tensor_copy(w1f[:, 0:LOW:HALF + 1], flat[:, 0:HALF * (NF + 1) - NF:NF + 1])
            nc.vector.tensor_copy(w1f[:, LOW + HALF:FW - 1:NF + 1],
                                  flat[:, HALF * (NF + 1):NF * NF:NF + 1]).then_inc(s_w1f, 1)

            def turn(b, f):
                dve.wait_ge(s_emb[f], 16 * (b + 1))
                nc.vector.transpose(embT[:, :, f], emb[:, f, :]).then_inc(s_turned, 1)

            def multiply(b, j):
                c = [n for n in range(NCH) if CH[n][0] <= j < CH[n][1]][0]
                at = tri(j) - tri(CH[c][0])
                dve.wait_ge(s_turned, NF * b + j + 1)
                last = nc.vector.tensor_tensor(pairs[c][:, :, at:at + j + 1], embT[:, :, 0:j + 1],
                                               embT[:, :, j:j + 1].to_broadcast([P, ROWS, j + 1]), ALU.mult)
                if j == CH[c][1] - 1:
                    last.then_inc(s_pairs, 1)

            def products(b, later):
                if later:
                    dve.wait_ge(s_pairs, NCH * b)
                for f in range(NF + 1):
                    if f < NF:
                        if later and f in CUTS:
                            dve.wait_ge(s_diag, 3 * b - 2 + CUTS.index(f))
                        turn(b, f)
                    if f > 0:
                        for c in range(NCH):
                            if later and f - 1 == CH[c][0]:
                                dve.wait_ge(s_T_ps, NG * b - NG + GOFF[c] + GROUPS[c])
                        multiply(b, f - 1)

            products(0, False)

            dve.wait_ge(s_F, NF)
            for c in range(NCH):
                for j in range(*CH[c]):
                    j0 = CH[c][0]
                    at = tri(j) - tri(j0)
                    w = w12t[c]
                    if j > j0:
                        nc.vector.memset(w[:, 0:j - j0, at:at + j + 1], 0.0)
                    nc.vector.tensor_copy(w[:, j - j0:NF - j0, at + j:at + j + 1], F[:, j:NF, pos(j, j):pos(j, j) + 1])
                    nc.vector.tensor_copy(w[:, NF - j0, at:at + j + 1], w1f[:, pos(j, 0):pos(j, j) + 1])
                    for l0, l1 in ((j, HALF), (max(j, HALF), NF)):
                        if j > 0 and l0 < l1:
                            step = pos(l0 + 1, 0) - pos(l0, 0) if l1 - l0 > 1 else 1
                            nc.vector.tensor_tensor(
                                w[:, l0 - j0:l1 - j0, at:at + j], F[:, l0:l1, pos(j, 0):pos(j, j)],
                                F[:, 0:j, pos(l0, j):pos(l1 - 1, j) + 1:step].rearrange("p i l -> p l i"), ALU.add)
            nc.vector.tensor_copy(w12t[0][:, 0:NF, CONST:CONST + 1], F[:, :, FW - 1:FW])
            nc.vector.tensor_copy(w12t[0][:, NF, CONST:CONST + 1], w1f[:, FW - 1:FW]).then_inc(s_fold, 1)
            dve.wait_ge(s_fold, 1)
            for c in range(NCH):
                for j in range(*CH[c]):
                    j0 = CH[c][0]
                    at = tri(j) - tri(j0)
                    w = w12t[c]
                    for l0, l1 in ((j + 1, HALF), (max(j + 1, HALF), NF)):
                        if l0 < l1:
                            step = NF if l0 >= HALF else HALF
                            rows = F[:, j, pos(l0, 0):pos(l1 - 1, 0) + step].rearrange("p (l i) -> p l i", i=step)
                            part = w[:, l0 - j0:l1 - j0, at:at + j + 1]
                            last = nc.vector.tensor_tensor(part, part, rows[:, :, 0:j + 1], ALU.add)
            last.then_inc(s_w12t, 1)

            with nc.vector.Fori(1, BLOCKS) as b:
                products(b, True)

        @block.tensor
        def _(pe):
            pe.wait_ge(s_ident, 1)
            pe.wait_ge(s_dense, 16)
            pe.wait_ge(s_set, 1)
            for b in range(BLOCKS):
                last = nc.tensor.transpose(h1_ps[0:ND + 1, b * P:(b + 1) * P], dense_nat[:, b, :], ident[:, :])
            last.then_inc(s_dT_ps, 1)
            pe.wait_ge(s_w2, 32)
            for n, batch in enumerate(W2_BATCHES):
                if n >= 2:
                    pe.wait_ge(s_w2t, n - 1)
                for l in batch:
                    last = nc.tensor.transpose(ring[n % 2][:, (l - batch[0]) * P:(l - batch[0] + 1) * P],
                                               w2_nat[:, :, l], ident[:, :])
                last.then_inc(s_w2t_ps, 1)
            pe.wait_ge(s_w1f, 1)
            for c in range(NF):
                pe.wait_ge(s_w2t, c // 4 + 1)
                if c >= 2:
                    pe.wait_ge(s_F, c - 1)
                nc.tensor.matmul(ring[2 + c % 2][:, 0:FW], w2t[:, c, :], w1f[:, :],
                                 start=True, stop=True).then_inc(s_F_ps, 1)

            def sums(b, c, first=False):
                pe.wait_ge(s_pairs, NCH * b + c + 1)
                if c == 0:
                    pe.wait_ge(s_diag, (len(CUTS) - 1) * (b + 1))
                for g in range(GROUPS[c]):
                    n = GOFF[c] + g
                    if not first or n >= RING:
                        pe.wait_ge(s_T, NG * b + n - RING + 1)
                    for i in range(PER[c]):
                        r = g * PER[c] + i
                        last = nc.tensor.matmul(
                            ring[n % RING][0:PAIRS[c], i * WIDE[c]:(i + 1) * WIDE[c]], pairs[c][:, r, :],
                            diag[:, r, CH[c][0]:NF + 1, :], start=True, stop=True)
                    last.then_inc(s_T_ps, 1)

            def weigh(b):
                for c in range(NCH):
                    pe.wait_ge(s_T, NG * b + GOFF[c] + GROUPS[c])
                    n = PAIRS[c]
                    at = LOFF[c] + LS[c] - 1
                    nc.tensor.matmul(z_ps[:, 0:P], w12[0:n, at, :], T[0:n, at, :], start=(c == 0), stop=(c == NCH - 1))
                for c in range(NCH):
                    n = PAIRS[c]
                    for at in range(LOFF[c], LOFF[c] + LS[c] - 1):
                        last = nc.tensor.matmul(z_ps[:, P:2 * P], w12[0:n, at, :], T[0:n, at, :],
                                                start=(at == 0), stop=(at == sum(LS) - 2))
                last.then_inc(s_z_ps, 1)

            def layer1(b, dense_block):
                pe.wait_ge(s_z, b + 1)
                for m in range(M1):
                    o = h1_ps[:, m * P:(m + 1) * P]
                    cols = slice(m * P, (m + 1) * P)
                    nc.tensor.matmul(o, top1d[:, cols], dense_block, start=True, stop=False)
                    nc.tensor.matmul(o, top1[:, 0, cols], z[:, 0, :], start=False, stop=False)
                    last = nc.tensor.matmul(o, top1[:, 1, cols], z[:, 1, :], start=False, stop=True)
                last.then_inc(s_h1_ps, 1)

            def layer2(b):
                pe.wait_ge(s_h1, b + 1)
                for m in range(M2):
                    for c in range(M1):
                        last = nc.tensor.matmul(h2_ps[:, m * P:(m + 1) * P], top2[:, c, m * P:(m + 1) * P], h1[:, c, :],
                                                start=(c == 0), stop=(c == M1 - 1))
                last.then_inc(s_h2_ps, 1)

            def layer3(b):
                pe.wait_ge(s_h2, b + 1)
                for m in range(M2):
                    last = nc.tensor.matmul(y_ps, top3[:, m:m + 1], h2[:, m, :], start=(m == 0), stop=(m == M2 - 1))
                last.then_inc(s_y_ps, 1)

            pe.wait_ge(s_F, NF)
            pe.wait_ge(s_set, 2)
            for c in range(NCH):
                sums(0, c, True)
            pe.wait_ge(s_w12t, 1)
            pe.wait_ge(s_dT, 1)
            for n, (c, ls) in enumerate(W12_BATCHES):
                if n >= 2:
                    pe.wait_ge(s_w12, n - 1)
                for i, l in enumerate(ls):
                    last = nc.tensor.transpose((turn_ps if n % 2 else h1_ps)[0:PAIRS[c], i * P:(i + 1) * P],
                                               w12t[c][:, l, :], ident[:, :])
                last.then_inc(s_w12_ps, 1)
            pe.wait_ge(s_w12, len(W12_BATCHES))
            pe.wait_ge(s_top, 16 * NTOP)
            with nc.tensor.Fori(0, BLOCKS - 1) as b:
                weigh(b)
                sums(b + 1, 0)
                layer1(b, denseT[:, bass.ds(b, 1), :].rearrange("p o n -> p (o n)"))
                sums(b + 1, 1)
                layer2(b)
                sums(b + 1, 2)
                layer3(b)
            weigh(BLOCKS - 1)
            layer1(BLOCKS - 1, denseT[:, BLOCKS - 1, :])
            layer2(BLOCKS - 1)
            layer3(BLOCKS - 1)


def kernel(**inputs):
    import numpy as np
    import concourse.bacc as bacc
    from concourse.bass_utils import run_bass_kernel_spmd as run

    nc = bacc.Bacc("TRN2", target_bir_lowering=False, num_devices=1)
    arrays, aps = {}, {}
    for name, value in inputs.items():
        a = np.ascontiguousarray(value)
        arrays[f"in_{name}"] = a
        aps[name] = nc.dram_tensor(f"in_{name}", a.shape, mybir.dt.from_np(a.dtype), kind="ExternalInput").ap()
    batch, fields = aps["ids"].shape
    out = nc.dram_tensor("out_y", (batch, 1), F32, kind="ExternalOutput").ap()
    dlrm_tower(nc, aps["dense_ctx"], aps["ids"], [aps[f"tbl_{f}"] for f in range(fields)],
               aps["W_top1"], aps["b_top1"], aps["W_top2"], aps["b_top2"], aps["W_top3"],
               aps["L0_rec_W1"], aps["L0_rec_b1"], aps["L0_rec_W2"], aps["L0_rec_b2"], out)
    return run(nc, [arrays], core_ids=[0]).results[0]["out_y"]
```

```python
from contextlib import ExitStack

import concourse.bass as bass
from concourse import mybir

F32 = mybir.dt.float32
I32 = mybir.dt.int32
ALU = mybir.AluOpType
ACT = mybir.ActivationFunctionType

P = 128
QUARTERS = 4
ROWS = P // QUARTERS


def tri(j):
    return j * (j + 1) // 2


def dlrm_tower(nc, dense, ids, tables, W_top1, b_top1, W_top2, b_top2, W_top3, W1, b1, W2, b2, out):
    BATCH, ND = dense.shape
    NF = ids.shape[1]
    K = tables[0].shape[1]
    H = W1.shape[0]
    H1, H2 = W_top2.shape
    BLOCKS = BATCH // P
    assert H == P and K == P // QUARTERS and BATCH % P == 0 and H1 % P == 0 and H2 % P == 0
    M1, M2 = H1 // P, H2 // P
    HALF = NF // 2
    assert NF == 2 * HALF and tri(HALF) + 1 <= 96
    NP = tri(HALF)
    ALONE = 96
    ROWS_OF = [ALONE, ALONE + HALF]
    NCH = 2
    NL = NF + 1
    WIDE = NL * QUARTERS
    PER = 4
    GROUPS = ROWS // PER
    NG = NCH * GROUPS
    RING = 4
    assert PER * WIDE <= 512 and NG % RING == 0

    SHORT, MOVED, OWN0, HOST = 7, 7, 8, 9
    assert tri(SHORT) <= 32 and tri(MOVED + 1) <= 64 and tri(HOST + 1) <= 64
    N_OWN = HALF - OWN0
    PER_CHUNK = N_OWN + HALF
    Z1 = NCH * PER_CHUNK
    N_CROSS = (HALF - 1) // QUARTERS
    assert N_CROSS * QUARTERS == HALF - 1
    N_SLOTS = Z1 + 2 + N_CROSS

    def own(c, l):
        return c * PER_CHUNK + l - OWN0

    def cross(c, m):
        return c * PER_CHUNK + N_OWN + m

    STAY = [(own(c, l), c, HALF * c + l, tri(l + 1)) for c in range(NCH) for l in range(OWN0, HALF) if l != HOST] + \
           [(cross(c, m), c, HALF * (1 - c) + m, NP + 1) for c in range(NCH) for m in range(SHORT, HALF)]
    MOVE = [(cross(c, m), c, HALF * (1 - c) + m, ALONE + tri(SHORT)) for c in range(NCH) for m in range(SHORT)] + \
           [(own(c, HOST), c, HALF * c + HOST, 64 + tri(MOVED + 1)) for c in range(NCH)]

    EARLY = 9
    PARTS = [0, NF // 3, 2 * NF // 3, NF]
    CUTS = [0, HALF, NF - 3, NF]

    LOW = HALF * HALF
    FW = LOW + (NF - HALF) * NF + 1

    with ExitStack() as ctx:
        def sb(name, shape, dt=F32):
            return ctx.enter_context(nc.sbuf_tensor(name, shape, dt))

        def bank(name):
            return ctx.enter_context(nc.psum_tensor(name, [P, 512], F32))

        def sem(name):
            return ctx.enter_context(nc.semaphore(name))

        idx = sb("idx", [P, BLOCKS, NF], I32)
        idx_now = sb("idx_now", [P, NF], I32)
        emb = sb("emb", [P, NF, K])
        embT = sb("embT", [P, ROWS, NF])
        diag = sb("diag", [P, ROWS, NF + 1, QUARTERS])
        pairs = [sb(f"pairs{c}", [P, ROWS, ROWS_OF[c]]) for c in range(NCH)]
        room_t = sb("room_t", [P, NCH, NL, P])
        T = [room_t[:, c, :, :] for c in range(NCH)]
        w2t = room_t[:, :, :, :].rearrange("p c l h -> p (c l) h")[:, 0:NF, :]
        across = sb("across", [P, N_CROSS, P])
        w1_nat = sb("w1_nat", [P, NF, NF])
        w1f = sb("w1f", [P, FW])
        F = sb("F", [P, NF, FW])
        FA = F[:, :, 0:LOW].rearrange("p c (a b) -> p c a b", b=HALF)
        FB = F[:, :, LOW:FW - 1].rearrange("p c (a b) -> p c a b", b=NF)
        room_w = sb("room_w", [P, max(N_SLOTS * P, H * NF)])
        w2_nat = room_w[:, 0:H * NF].rearrange("p (i l) -> p i l", l=NF)
        w12 = room_w[:, 0:N_SLOTS * P].rearrange("p (s h) -> p s h", h=P)
        w12t = sb("w12t", [P, N_SLOTS, P])
        zero = sb("zero", [P, 1])
        one = sb("one", [P, 1])
        top1 = sb("top1", [P, 2, H1])
        top1d = sb("top1d", [ND + 1, H1])
        top2 = sb("top2", [P, M1, H2])
        top3 = sb("top3", [P, M2])
        b2_sb = sb("b2_sb", [P, 1])
        kb2 = sb("kb2", [P, 1])
        bt2 = sb("bt2", [P, M2])
        dense_nat = sb("dense_nat", [P, BLOCKS, ND + 1])
        denseT = sb("denseT", [ND + 1, BLOCKS, P])
        ident = sb("ident", [P, P])
        z = sb("z", [P, 2, P])
        h1 = sb("h1", [P, M1, P])
        h2 = sb("h2", [P, M2, P])
        y = sb("y", [1, P])

        ring = [bank(f"ring{n}") for n in range(RING)]
        z_ps = bank("z_ps")
        h1_ps = bank("h1_ps")
        h2_ps = bank("h2_ps")
        turn_ps = [h1_ps, bank("turn_ps")]
        y_ps = h2_ps[0:1, M2 * P:(M2 + 1) * P]

        s_ids = sem("s_ids")
        s_w1 = sem("s_w1")
        s_w2 = sem("s_w2")
        s_dense = sem("s_dense")
        s_top = sem("s_top")
        s_ident0 = sem("s_ident0")
        s_ident = sem("s_ident")
        s_idx = sem("s_idx")
        s_emb = [sem(f"s_emb{f}") for f in range(NF)]
        s_room = sem("s_room")
        s_set = sem("s_set")
        s_clear = sem("s_clear")
        s_w1f0 = sem("s_w1f0")
        s_w1f = sem("s_w1f")
        s_turned = sem("s_turned")
        s_pairs = sem("s_pairs")
        s_fold = sem("s_fold")
        s_packed = sem("s_packed")
        s_w12t = sem("s_w12t")
        s_kb2 = sem("s_kb2")
        s_diag = sem("s_diag")
        s_dT_ps = sem("s_dT_ps")
        s_dT = sem("s_dT")
        s_w2t_ps = sem("s_w2t_ps")
        s_w2t = sem("s_w2t")
        s_F_ps = sem("s_F_ps")
        s_F = sem("s_F")
        s_w12_ps = sem("s_w12_ps")
        s_w12 = sem("s_w12")
        s_T_ps = sem("s_T_ps")
        s_T = sem("s_T")
        s_z_ps = sem("s_z_ps")
        s_z = sem("s_z")
        s_h1_ps = sem("s_h1_ps")
        s_h1 = sem("s_h1")
        s_h2_ps = sem("s_h2_ps")
        s_h2 = sem("s_h2")
        s_y_ps = sem("s_y_ps")
        s_y = sem("s_y")
        s_out = sem("s_out")

        W12_BATCHES = [range(n, min(n + 4, N_SLOTS)) for n in range(0, N_SLOTS, 4)]
        W2_BATCHES = [range(n, min(n + 4, NF)) for n in range(0, NF, 4)]
        NTOP = 7

        block = ctx.enter_context(nc.Block())

        @block.sync
        def _(sp):
            sp.dma_start(idx[:, :, :], ids.rearrange("(q p) f -> p q f", p=P)).then_inc(s_ids, 16)
            sp.dma_start(room_w[0:P // 2, 0:H * NF], W2.rearrange("h i l -> h (i l)")[0:P // 2, :]).then_inc(s_w2, 16)
            sp.dma_start(w1_nat[:, :, :], W1).then_inc(s_w1, 16)
            sp.dma_start(w1f[:, FW - 1:FW], b1.rearrange("(p o) -> p o", o=1)).then_inc(s_w1, 16)
            sp.dma_start(dense_nat[:, :, 0:ND], dense.rearrange("(q p) d -> p q d", p=P)).then_inc(s_dense, 16)
            sp.dma_start(top1[:, :, :], W_top1[0:2 * P, :].rearrange("(c p) n -> p c n", p=P)).then_inc(s_top, 16)
            sp.dma_start(top1d[0:ND, :], W_top1[2 * P:2 * P + ND, :]).then_inc(s_top, 16)
            sp.dma_start(top1d[ND:ND + 1, :], b_top1.rearrange("(o n) -> o n", o=1)).then_inc(s_top, 16)
            sp.dma_start(top2[:, :, :], W_top2.rearrange("(c p) n -> p c n", p=P)).then_inc(s_top, 16)
            sp.dma_start(b2_sb[:, :], b2.rearrange("(p o) -> p o", o=1)).then_inc(s_top, 16)
            with nc.allow_non_contiguous_dma(reason="a few hundred words"):
                sp.dma_start(bt2[:, :], b_top2.rearrange("(c p) -> p c", p=P)).then_inc(s_top, 16)
                sp.dma_start(top3[:, :], W_top3.rearrange("(c p) o -> p (c o)", p=P)).then_inc(s_top, 16)
            with nc.sync.Fori(0, BLOCKS) as b:
                sp.wait_ge(s_y, b + 1)
                sp.dma_start(out[bass.ds(b * P, P), :].rearrange("p o -> o p"), y[:, :]).then_inc(s_out, 16)
            sp.wait_ge(s_out, 16 * BLOCKS)

        @block.gpsimd
        def _(pool):
            nc.gpsimd.memset(ident[:, :], 0.0).then_inc(s_ident0, 1)
            pool.wait_ge(s_ident0, 1)
            nc.gpsimd.affine_select(out=ident[:, :], in_=ident[:, :], compare_op=ALU.not_equal, fill=1.0, base=0,
                                    pattern=[[-1, P]], channel_multiplier=1).then_inc(s_ident, 1)
            pool.wait_ge(s_ids, 16)

            def gathers(b, later):
                for part in range(len(PARTS) - 1):
                    f0, f1 = PARTS[part], PARTS[part + 1]
                    if later:
                        pool.wait_ge(s_turned, b * NF - NF + f1)
                        pool.sem_inc(s_room, 1)
                    ids_now = (idx[:, bass.ds(b, 1), f0:f1].rearrange("p o f -> p (o f)") if later
                               else idx[:, b, f0:f1])
                    nc.gpsimd.tensor_copy(idx_now[:, f0:f1], ids_now).then_inc(s_idx, 1)
                    pool.wait_ge(s_idx, b * (len(PARTS) - 1) + part + 1)
                    if later:
                        pool.sem_inc(s_room, 1)
                    for f in range(f0, f1):
                        nc.gpsimd.indirect_dma_start(emb[:, f, :], None, tables[f],
                                                     bass.IndirectOffsetOnAxis(ap=idx_now[:, f:f + 1], axis=0)
                                                     ).then_inc(s_emb[f], 16)

            gathers(0, False)
            with nc.gpsimd.Fori(1, BLOCKS) as b:
                gathers(b, True)

        @block.scalar
        def _(act):
            act.dma_start(room_w[P // 2:P, 0:H * NF], W2.rearrange("h i l -> h (i l)")[P // 2:P, :]).then_inc(s_w2, 16)
            act.wait_ge(s_set, 1)
            nc.scalar.copy(diag[:, :, :, :].rearrange("p r l q -> p (r l q)"),
                           zero[:, 0:1].to_broadcast([P, ROWS * NL * QUARTERS])).then_inc(s_clear, 1)
            act.wait_ge(s_clear, 1)
            for q in range(QUARTERS):
                last = nc.scalar.copy(diag[q * ROWS:(q + 1) * ROWS, :, NF, q],
                                      one[q * ROWS:(q + 1) * ROWS, 0:1].to_broadcast([ROWS, ROWS]))
            last.then_inc(s_clear, 1)
            act.wait_ge(s_dT_ps, 1)
            nc.scalar.copy(denseT[:, :, :].rearrange("p b (r q) -> p b q r", q=QUARTERS),
                           h1_ps[0:ND + 1, :].rearrange("p (b q r) -> p b q r", b=BLOCKS, q=QUARTERS)).then_inc(s_dT, 1)
            for n, batch in enumerate(W2_BATCHES):
                act.wait_ge(s_w2t_ps, n + 1)
                nc.scalar.copy(w2t[:, batch[0]:batch[-1] + 1, :],
                               ring[n % 2][:, 0:len(batch) * P].rearrange("p (l h) -> p l h", h=P)).then_inc(s_w2t, 1)
            for c in range(NF):
                act.wait_ge(s_F_ps, c + 1)
                nc.scalar.copy(F[:, c, :], ring[2 + c % 2][:, 0:FW]).then_inc(s_F, 1)
            act.wait_ge(s_top, 16 * NTOP)
            nc.scalar.mul(kb2[:, :], b2_sb[:, :], float(K)).then_inc(s_kb2, 1)

            def spread(b):
                for part in range(len(CUTS) - 1):
                    f0, f1 = CUTS[part], CUTS[part + 1]
                    act.wait_ge(s_turned, NF * b + f1)
                    for q in range(QUARTERS):
                        quarter = slice(q * ROWS, (q + 1) * ROWS)
                        last = nc.scalar.copy(diag[quarter, :, f0:f1, q], embT[quarter, :, f0:f1])
                    last.then_inc(s_diag, 1)

            def keep_T(b, first, end):
                for n in range(first, end):
                    c, g = divmod(n, GROUPS)
                    act.wait_ge(s_T_ps, NG * b + n + 1)
                    rows = ROWS_OF[c]
                    src = ring[n % RING][0:rows, 0:PER * WIDE].rearrange("p (r l q) -> p l r q", r=PER, q=QUARTERS)
                    dst = T[c][0:rows, :, g * PER * QUARTERS:(g + 1) * PER * QUARTERS].rearrange(
                        "p l (r q) -> p l r q", q=QUARTERS)
                    nc.scalar.copy(dst, src).then_inc(s_T, 1)

            def keep_z(b):
                act.wait_ge(s_z_ps, b + 1)
                nc.scalar.copy(z[:, 0, :], z_ps[:, 0:P])
                nc.scalar.activation(z[:, 1, :], z_ps[:, P:2 * P], ACT.Identity, bias=kb2[:, 0:1]).then_inc(s_z, 1)

            def relu1(b):
                act.wait_ge(s_h1_ps, b + 1)
                nc.scalar.activation(h1[:, :, :], h1_ps[:, 0:M1 * P].rearrange("p (m n) -> p m n", n=P),
                                     ACT.Relu).then_inc(s_h1, 1)

            def relu2(b):
                act.wait_ge(s_h2_ps, b + 1)
                for m in range(M2):
                    last = nc.scalar.activation(h2[:, m, :], h2_ps[:, m * P:(m + 1) * P], ACT.Relu, bias=bt2[:, m:m + 1])
                last.then_inc(s_h2, 1)

            def keep_y(b, later=True):
                act.wait_ge(s_y_ps, b + 1)
                if later:
                    act.wait_ge(s_out, 16 * b)
                nc.scalar.copy(y[:, :].rearrange("p (q r) -> p r q", q=QUARTERS),
                               y_ps.rearrange("p (r q) -> p r q", q=QUARTERS)).then_inc(s_y, 1)

            spread(0)
            keep_T(0, 0, NG)
            for n, slots in enumerate(W12_BATCHES):
                act.wait_ge(s_w12_ps, n + 1)
                nc.scalar.copy(w12[:, slots[0]:slots[-1] + 1, :], turn_ps[n % 2][:, 0:len(slots) * P].rearrange(
                    "p (s h) -> p s h", h=P)).then_inc(s_w12, 1)
            act.wait_ge(s_kb2, 1)

            def tail_of(b, later=True):
                spread(b + 1)
                keep_z(b)
                keep_T(b + 1, 0, GROUPS)
                relu1(b)
                keep_T(b + 1, GROUPS, GROUPS + GROUPS // 2)
                relu2(b)
                keep_T(b + 1, GROUPS + GROUPS // 2, NG)
                keep_y(b, later)

            tail_of(0, False)
            with nc.scalar.Fori(1, BLOCKS - 1) as b:
                tail_of(b)
            keep_z(BLOCKS - 1)
            relu1(BLOCKS - 1)
            relu2(BLOCKS - 1)
            keep_y(BLOCKS - 1)

        @block.vector
        def _(dve):
            nc.vector.memset(zero[:, :], 0.0)
            nc.vector.memset(one[:, :], 1.0).then_inc(s_set, 1)
            nc.vector.memset(dense_nat[:, :, ND:ND + 1], 1.0)
            nc.vector.memset(across[:, :, :], 0.0)
            for c in range(NCH):
                nc.vector.memset(pairs[c][:, :, NP:NP + 1], 1.0)
                nc.vector.memset(pairs[c][:, :, NP + 1:ALONE], 0.0)
            nc.vector.memset(w12t[:, :, :], 0.0).then_inc(s_set, 1)

            dve.wait_ge(s_w1, 32)
            low = w1f[:, 0:LOW].rearrange("p (a b) -> p a b", b=HALF)
            high = w1f[:, LOW:FW - 1].rearrange("p (a b) -> p a b", b=NF)
            turned = w1_nat[:, :, :].rearrange("p a b -> p b a")
            nc.vector.tensor_tensor(low, w1_nat[:, 0:HALF, 0:HALF], turned[:, 0:HALF, 0:HALF], ALU.add)
            nc.vector.tensor_tensor(high, w1_nat[:, HALF:NF, :], turned[:, HALF:NF, :], ALU.add).then_inc(s_w1f0, 1)
            flat = w1_nat[:, :, :].rearrange("p a b -> p (a b)")
            dve.wait_ge(s_w1f0, 1)
            nc.vector.tensor_copy(w1f[:, 0:LOW:HALF + 1], flat[:, 0:HALF * (NF + 1) - NF:NF + 1])
            nc.vector.tensor_copy(w1f[:, LOW + HALF:FW - 1:NF + 1],
                                  flat[:, HALF * (NF + 1):NF * NF:NF + 1]).then_inc(s_w1f, 1)

            dve.wait_ge(s_w1f, 1)
            dve.wait_ge(s_set, 2)
            for c, rows in enumerate((low, high)):
                for j in range(HALF):
                    nc.vector.tensor_copy(w12t[:, Z1 + c, tri(j):tri(j + 1)], rows[:, j, HALF * c:HALF * c + j + 1])
            nc.vector.tensor_copy(w12t[:, Z1, NP:NP + 1], w1f[:, FW - 1:FW])
            nc.vector.tensor_copy(w12t[:, Z1, ALONE:ALONE + HALF], high[:, HALF - 1, 0:HALF])
            for q in range(QUARTERS):
                nc.vector.tensor_copy(w12t[:, Z1 + 2:N_SLOTS, q * ROWS:q * ROWS + HALF],
                                      high[:, q * N_CROSS:(q + 1) * N_CROSS, 0:HALF])

            def turn(b, f):
                dve.wait_ge(s_emb[f], 16 * (b + 1))
                nc.vector.transpose(embT[:, :, f], emb[:, f, :]).then_inc(s_turned, 1)

            def multiply(b, f):
                c, j = divmod(f, HALF)
                f0 = HALF * c
                dve.wait_ge(s_turned, NF * b + f + 1)
                last = nc.vector.tensor_tensor(pairs[c][:, :, tri(j):tri(j + 1)], embT[:, :, f0:f + 1],
                                               embT[:, :, f:f + 1].to_broadcast([P, ROWS, j + 1]), ALU.mult)
                if j == HALF - 1:
                    last.then_inc(s_pairs, 1)

            def products(b, c, later, first=0, end=HALF):
                if later and c == 0:
                    dve.wait_ge(s_pairs, NCH * b)
                for j in range(first, end + (end == HALF)):
                    f = HALF * c + j
                    if j < HALF:
                        if later and f in CUTS:
                            dve.wait_ge(s_diag, 3 * b - 2 + CUTS.index(f))
                        turn(b, f)
                    if j == 0:
                        if later:
                            dve.wait_ge(s_T_ps, NG * b - NG + GROUPS * (c + 1))
                        if c == 1:
                            nc.vector.tensor_copy(pairs[1][:, :, ALONE:ALONE + HALF], embT[:, :, 0:HALF])
                    else:
                        multiply(b, f - 1)

            def pack(b):
                dve.wait_ge(s_T, NG * b + GROUPS)
                nc.vector.tensor_copy(T[0][ALONE:ALONE + tri(SHORT), HALF:HALF + SHORT, :], T[0][0:tri(SHORT), 0:SHORT, :])
                nc.vector.tensor_copy(T[0][64:64 + tri(MOVED + 1), HOST, :],
                                      T[0][0:tri(MOVED + 1), MOVED, :]).then_inc(s_packed, 1)
                dve.wait_ge(s_T, NG * b + NG)
                alone = T[1][ALONE:ALONE + HALF, HALF:NF, :]
                for q in range(QUARTERS):
                    nc.vector.tensor_copy(across[q * ROWS:q * ROWS + HALF, :, :], alone[:, q * N_CROSS:(q + 1) * N_CROSS, :])
                nc.vector.tensor_copy(T[0][ALONE:ALONE + HALF, NF, :], alone[:, HALF - 1, :]).then_inc(s_packed, 1)
                nc.vector.tensor_copy(T[1][ALONE:ALONE + tri(SHORT), 0:SHORT, :],
                                      T[1][0:tri(SHORT), HALF:HALF + SHORT, :]).then_inc(s_packed, 1)
                dve.wait_ge(s_packed, 4 * b + 2)
                nc.vector.tensor_copy(T[1][64:64 + tri(MOVED + 1), HALF + HOST, :],
                                      T[1][0:tri(MOVED + 1), HALF + MOVED, :]).then_inc(s_packed, 1)

            def own_rows(c, l0, l1, j, n):
                at = tri(j)
                if l1 <= SHORT:
                    return w12t[:, cross(c, l0):cross(c, l1), ALONE + at:ALONE + at + n]
                if l0 == MOVED:
                    return w12t[:, own(c, HOST):own(c, HOST) + 1, 64 + at:64 + at + n]
                return w12t[:, own(c, l0):own(c, l1), at:at + n]

            def ranges(l0):
                return [(max(a, l0), b) for a, b in ((0, SHORT), (MOVED, OWN0), (OWN0, HALF)) if max(a, l0) < b]

            def join_own(c, step):
                R, f0 = (FA, FB)[c], HALF * c
                for j in range(HALF):
                    if step == 0:
                        last = nc.vector.tensor_copy(own_rows(c, j, j + 1, j, j + 1), R[:, f0 + j, j:j + 1, f0:f0 + j + 1])
                        for l0, l1 in ranges(j + 1):
                            last = nc.vector.tensor_tensor(
                                own_rows(c, l0, l1, j, j + 1), R[:, f0 + l0:f0 + l1, j, f0:f0 + j + 1],
                                R[:, f0 + j, l0:l1, f0:f0 + j + 1], ALU.add)
                    elif j > 0:
                        for l0, l1 in ranges(j):
                            rows = own_rows(c, l0, l1, j, j)
                            last = nc.vector.tensor_tensor(
                                rows, rows, R[:, f0:f0 + j, l0:l1, f0 + j].rearrange("p i l -> p l i"), ALU.add)
                return last

            def join_cross(c, step):
                for j in range(HALF):
                    at = tri(j)
                    rows = w12t[:, cross(c, 0):cross(c, HALF), at:at + j + 1]
                    if step == 0 and c == 0:
                        last = nc.vector.tensor_tensor(rows, FA[:, HALF:NF, j, 0:j + 1], FB[:, j, :, 0:j + 1], ALU.add)
                    elif step == 0:
                        last = nc.vector.tensor_tensor(
                            rows, FB[:, 0:HALF, j, HALF:HALF + j + 1],
                            FB[:, HALF + j, 0:j + 1, 0:HALF].rearrange("p i l -> p l i"), ALU.add)
                    elif j > 0:
                        third = (FB[:, 0:j, :, j] if c == 0 else FB[:, HALF:HALF + j, j, 0:HALF])
                        rows = rows[:, :, 0:j]
                        last = nc.vector.tensor_tensor(rows, rows, third.rearrange("p i l -> p l i"), ALU.add)
                if step == 0:
                    other = slice(HALF * (1 - c), HALF * (2 - c))
                    last = nc.vector.tensor_copy(w12t[:, cross(c, 0):cross(c, HALF), NP:NP + 1], F[:, other, FW - 1:FW])
                return last

            products(0, 0, False)
            products(0, 1, False, 0, EARLY)
            dve.wait_ge(s_F, HALF)
            join_own(0, 0).then_inc(s_fold, 1)
            dve.wait_ge(s_fold, 1)
            join_own(0, 1)
            products(0, 1, False, EARLY)
            dve.wait_ge(s_F, NF)
            join_cross(0, 0)
            join_cross(1, 0)
            join_own(1, 0).then_inc(s_fold, 1)
            dve.wait_ge(s_fold, 2)
            join_cross(0, 1)
            join_cross(1, 1)
            join_own(1, 1).then_inc(s_w12t, 1)

            with nc.vector.Fori(1, BLOCKS) as b:
                products(b, 0, True)
                pack(b - 1)
                products(b, 1, True)
            pack(BLOCKS - 1)

        @block.tensor
        def _(pe):
            pe.wait_ge(s_ident, 1)
            pe.wait_ge(s_dense, 16)
            pe.wait_ge(s_set, 2)
            for b in range(BLOCKS):
                last = nc.tensor.transpose(h1_ps[0:ND + 1, b * P:(b + 1) * P], dense_nat[:, b, :], ident[:, :])
            last.then_inc(s_dT_ps, 1)
            pe.wait_ge(s_w2, 32)
            for n, batch in enumerate(W2_BATCHES):
                if n >= 2:
                    pe.wait_ge(s_w2t, n - 1)
                for l in batch:
                    last = nc.tensor.transpose(ring[n % 2][:, (l - batch[0]) * P:(l - batch[0] + 1) * P],
                                               w2_nat[:, :, l], ident[:, :])
                last.then_inc(s_w2t_ps, 1)
            pe.wait_ge(s_w1f, 1)
            for c in range(NF):
                pe.wait_ge(s_w2t, c // 4 + 1)
                if c >= 2:
                    pe.wait_ge(s_F, c - 1)
                nc.tensor.matmul(ring[2 + c % 2][:, 0:FW], w2t[:, c, :], w1f[:, :],
                                 start=True, stop=True).then_inc(s_F_ps, 1)

            def sums(b, first, end, fresh=False):
                for n in range(first, end):
                    c, g = divmod(n, GROUPS)
                    if n == first:
                        pe.wait_ge(s_pairs, NCH * b + c + 1)
                    if n == 0:
                        pe.wait_ge(s_diag, (len(CUTS) - 1) * (b + 1))
                    if not fresh or n >= RING:
                        pe.wait_ge(s_T, NG * b + n - RING + 1)
                    for i in range(PER):
                        r = g * PER + i
                        last = nc.tensor.matmul(ring[n % RING][0:ROWS_OF[c], i * WIDE:(i + 1) * WIDE], pairs[c][:, r, :],
                                                diag[:, r, :, :], start=True, stop=True)
                    last.then_inc(s_T_ps, 1)

            def weigh(b):
                o = z_ps[:, P:2 * P]
                pe.wait_ge(s_T, NG * b + NG)
                for i, (slot, c, l, k) in enumerate(STAY):
                    nc.tensor.matmul(o, w12[0:k, slot, :], T[c][0:k, l, :], start=(i == 0), stop=False)
                pe.wait_ge(s_packed, 4 * b + 4)
                for i, (slot, c, l, k) in enumerate(MOVE):
                    nc.tensor.matmul(o, w12[0:k, slot, :], T[c][0:k, l, :], start=False, stop=(i == len(MOVE) - 1))
                o = z_ps[:, 0:P]
                k = ALONE + HALF
                nc.tensor.matmul(o, w12[0:k, Z1, :], T[0][0:k, NF, :], start=True, stop=False)
                nc.tensor.matmul(o, w12[0:NP, Z1 + 1, :], T[1][0:NP, NF, :], start=False, stop=False)
                for i in range(N_CROSS):
                    last = nc.tensor.matmul(o, w12[0:k, Z1 + 2 + i, :], across[0:k, i, :], start=False,
                                            stop=(i == N_CROSS - 1))
                last.then_inc(s_z_ps, 1)

            def layer1(b, dense_block):
                pe.wait_ge(s_z, b + 1)
                for m in range(M1):
                    o = h1_ps[:, m * P:(m + 1) * P]
                    cols = slice(m * P, (m + 1) * P)
                    nc.tensor.matmul(o, top1d[:, cols], dense_block, start=True, stop=False)
                    nc.tensor.matmul(o, top1[:, 0, cols], z[:, 0, :], start=False, stop=False)
                    last = nc.tensor.matmul(o, top1[:, 1, cols], z[:, 1, :], start=False, stop=True)
                last.then_inc(s_h1_ps, 1)

            def layer2(b):
                pe.wait_ge(s_h1, b + 1)
                for m in range(M2):
                    for c in range(M1):
                        last = nc.tensor.matmul(h2_ps[:, m * P:(m + 1) * P], top2[:, c, m * P:(m + 1) * P], h1[:, c, :],
                                                start=(c == 0), stop=(c == M1 - 1))
                last.then_inc(s_h2_ps, 1)

            def layer3(b):
                pe.wait_ge(s_h2, b + 1)
                for m in range(M2):
                    last = nc.tensor.matmul(y_ps, top3[:, m:m + 1], h2[:, m, :], start=(m == 0), stop=(m == M2 - 1))
                last.then_inc(s_y_ps, 1)

            pe.wait_ge(s_F, NF)
            pe.wait_ge(s_clear, 2)
            sums(0, 0, GROUPS, True)
            sums(0, GROUPS, NG, True)
            pe.wait_ge(s_w12t, 1)
            pe.wait_ge(s_dT, 1)
            for n, slots in enumerate(W12_BATCHES):
                if n >= 2:
                    pe.wait_ge(s_w12, n - 1)
                for i, slot in enumerate(slots):
                    last = nc.tensor.transpose(turn_ps[n % 2][:, i * P:(i + 1) * P], w12t[:, slot, :], ident[:, :])
                last.then_inc(s_w12_ps, 1)
            pe.wait_ge(s_w12, len(W12_BATCHES))
            pe.wait_ge(s_top, 16 * NTOP)
            with nc.tensor.Fori(0, BLOCKS - 1) as b:
                weigh(b)
                sums(b + 1, 0, GROUPS)
                layer1(b, denseT[:, bass.ds(b, 1), :].rearrange("p o n -> p (o n)"))
                sums(b + 1, GROUPS, GROUPS + GROUPS // 2)
                layer2(b)
                sums(b + 1, GROUPS + GROUPS // 2, NG)
                layer3(b)
            weigh(BLOCKS - 1)
            layer1(BLOCKS - 1, denseT[:, BLOCKS - 1, :])
            layer2(BLOCKS - 1)
            layer3(BLOCKS - 1)


def kernel(**inputs):
    import numpy as np
    import concourse.bacc as bacc
    from concourse.bass_utils import run_bass_kernel_spmd as run

    nc = bacc.Bacc("TRN2", target_bir_lowering=False, num_devices=1)
    arrays, aps = {}, {}
    for name, value in inputs.items():
        a = np.ascontiguousarray(value)
        arrays[f"in_{name}"] = a
        aps[name] = nc.dram_tensor(f"in_{name}", a.shape, mybir.dt.from_np(a.dtype), kind="ExternalInput").ap()
    batch, fields = aps["ids"].shape
    out = nc.dram_tensor("out_y", (batch, 1), F32, kind="ExternalOutput").ap()
    dlrm_tower(nc, aps["dense_ctx"], aps["ids"], [aps[f"tbl_{f}"] for f in range(fields)],
               aps["W_top1"], aps["b_top1"], aps["W_top2"], aps["b_top2"], aps["W_top3"],
               aps["L0_rec_W1"], aps["L0_rec_b1"], aps["L0_rec_W2"], aps["L0_rec_b2"], out)
    return run(nc, [arrays], core_ids=[0]).results[0]["out_y"]
```

```python
from contextlib import ExitStack

import concourse.bass as bass
from concourse import mybir

F32 = mybir.dt.float32
I32 = mybir.dt.int32
ALU = mybir.AluOpType
ACT = mybir.ActivationFunctionType

P = 128
QUARTERS = 4
ROWS = P // QUARTERS


def tri(j):
    return j * (j + 1) // 2


def dlrm_tower(nc, dense, ids, tables, W_top1, b_top1, W_top2, b_top2, W_top3, W1, b1, W2, b2, out):
    BATCH, ND = dense.shape
    NF = ids.shape[1]
    K = tables[0].shape[1]
    H = W1.shape[0]
    H1, H2 = W_top2.shape
    BLOCKS = BATCH // P
    assert H == P and K == P // QUARTERS and BATCH % P == 0 and H1 % P == 0 and H2 % P == 0
    M1, M2 = H1 // P, H2 // P
    HALF = NF // 2
    assert NF == 2 * HALF and tri(HALF) + 1 <= 96
    NP = tri(HALF)
    ALONE = 96
    ROWS_OF = [ALONE, ALONE + HALF]
    NCH = 2
    NL = NF + 1
    WIDE = NL * QUARTERS
    PER = 4
    GROUPS = ROWS // PER
    NG = NCH * GROUPS
    RING = 4
    assert PER * WIDE <= 512 and NG % RING == 0

    OWN = [9, 11, 12]
    N_OWN = len(OWN)
    SHORT = 7
    MOVES = [(7, 0, 32, N_OWN + 7, ALONE), (7, 32, tri(8), N_OWN + 8, ALONE),
             (10, 0, 32, N_OWN + 9, ALONE), (10, 32, 64, N_OWN + 10, ALONE), (10, 64, tri(11), N_OWN + 11, ALONE),
             (8, 0, tri(9), 0, 64)]
    assert HALF == OWN[-1] + 1 and tri(SHORT) <= 32 and tri(OWN[0] + 1) <= 64
    assert sorted(OWN + list(range(SHORT)) + list({move[0] for move in MOVES})) == list(range(HALF))
    assert max(tri(l + 1) for l in OWN[1:]) < ALONE
    PACKS = 5
    PER_CHUNK = N_OWN + HALF
    N_CROSS = (HALF - 1) // QUARTERS
    assert N_CROSS * QUARTERS == HALF - 1
    N_Z1 = NCH + N_CROSS
    N_SLOTS = N_Z1 + NCH * PER_CHUNK

    def slot_of(c, s):
        return N_Z1 + c * PER_CHUNK + s

    def l_of(c, s):
        return HALF * c + OWN[s] if s < N_OWN else HALF * (1 - c) + s - N_OWN

    def rows_of(s):
        ends = [row + end - first for _, first, end, slot, row in MOVES if slot == s]
        if N_OWN <= s < N_OWN + SHORT:
            ends = [ALONE + tri(SHORT)]
        return max(ends + [tri(OWN[s] + 1) if s < N_OWN else NP + 1])

    STAY = [s for s in range(PER_CHUNK) if rows_of(s) < ALONE]
    MOVE = [s for s in range(PER_CHUNK) if rows_of(s) >= ALONE]

    FIRST, SECOND = 3, 9
    EARLY = 4
    JOIN_A = [(0, 0, 5), (0, 5, HALF), (1, 1, HALF), (2, 0, 0)]
    LATE = 2
    SPREAD_AT = [18, 19, 20, 21, 22, 23, 24, 25]
    BLOCK_1 = [(range(HALF), range(9)), (range(HALF, 20), range(9, HALF)), (range(20, NF), [])]
    CUTS = [[HALF, 20, 23, NF], [0, HALF, 20, 23, NF]]
    NCUT = [len(cuts) - 1 for cuts in CUTS]
    PARTS = [0, HALF, NF]
    SPREAD_TO = [HALF, 19, 23, NF - 1]
    PACK_AT = [8, 11]

    SAME = HALF * (HALF + 1)
    FW = SAME + HALF * HALF + 1

    with ExitStack() as ctx:
        def sb(name, shape, dt=F32):
            return ctx.enter_context(nc.sbuf_tensor(name, shape, dt))

        def bank(name):
            return ctx.enter_context(nc.psum_tensor(name, [P, 512], F32))

        def sem(name):
            return ctx.enter_context(nc.semaphore(name))

        idx = sb("idx", [P, BLOCKS + 1, NF], I32)
        idx_now = sb("idx_now", [P, NF], I32)
        emb = sb("emb", [P, NF, K])
        embT = sb("embT", [P, ROWS, NF])
        diag = sb("diag", [P, ROWS, NF + 1, QUARTERS])
        pairs = [sb(f"pairs{c}", [P, ROWS, ROWS_OF[c]]) for c in range(NCH)]
        room_t = sb("room_t", [P, NCH, NL, P])
        T = [room_t[:, c, :, :] for c in range(NCH)]
        w2t = room_t[:, :, :, :].rearrange("p c l h -> p (c l) h")[:, 0:NF, :]
        across = sb("across", [P, N_CROSS, P])
        w1_nat = sb("w1_nat", [P, NF, NF])
        w1f = sb("w1f", [P, FW])
        F = sb("F", [P, NF, FW])
        same = F[:, :, 0:SAME].rearrange("p c (r s) -> p c r s", s=HALF + 1)
        mixed = F[:, :, SAME:FW - 1].rearrange("p c (b a) -> p c b a", a=HALF)
        room_w = sb("room_w", [P, max(N_SLOTS * P, H * NF)])
        w2_nat = room_w[:, 0:H * NF].rearrange("p (i l) -> p i l", l=NF)
        w12 = room_w[:, 0:N_SLOTS * P].rearrange("p (s h) -> p s h", h=P)
        w12t = sb("w12t", [P, N_SLOTS, P])
        own_w = sb("own_w", [P, HALF, NP])
        zero = sb("zero", [P, 1])
        one = sb("one", [P, 1])
        top1 = sb("top1", [P, 2, H1])
        top1d = sb("top1d", [ND + 1, H1])
        top2 = sb("top2", [P, M1, H2])
        top3 = sb("top3", [P, M2])
        b2_sb = sb("b2_sb", [P, 1])
        kb2 = sb("kb2", [P, 1])
        bt2 = sb("bt2", [P, M2])
        dense_nat = sb("dense_nat", [P, BLOCKS, ND + 1])
        denseT = sb("denseT", [ND + 1, BLOCKS, P])
        ident = sb("ident", [P, P])
        z = sb("z", [P, 2, P])
        h1 = sb("h1", [P, M1, P])
        h2 = sb("h2", [P, M2, P])
        y = sb("y", [1, P])

        ring = [bank(f"ring{n}") for n in range(RING)]
        z2_ps = bank("z2_ps")
        z1_ps = bank("z1_ps")
        h1_ps = [bank("h1_ps0"), bank("h1_ps1")]
        turn_ps = [z2_ps, z1_ps]
        assert M1 % 2 == 0 and M1 // 2 * P <= 512 and M2 == 2
        M1H = M1 // 2
        h2_at = [z2_ps[:, 0:P], z1_ps[:, 0:P]]
        y_ps = z2_ps[0:1, P:2 * P]

        s_ids = sem("s_ids")
        s_more_ids = sem("s_more_ids")
        s_w1 = sem("s_w1")
        s_w2 = sem("s_w2")
        s_dense = sem("s_dense")
        s_top = sem("s_top")
        s_ident0 = sem("s_ident0")
        s_ident = sem("s_ident")
        s_idx = sem("s_idx")
        s_emb = [sem(f"s_emb{f}") for f in range(NF)]
        s_room = sem("s_room")
        s_set = sem("s_set")
        s_clear = sem("s_clear")
        s_w1f0 = sem("s_w1f0")
        s_w1f = sem("s_w1f")
        s_turned = sem("s_turned")
        s_pairs = sem("s_pairs")
        s_fold = sem("s_fold")
        s_packed = sem("s_packed")
        s_w12t = sem("s_w12t")
        s_kb2 = sem("s_kb2")
        s_diag_act = sem("s_diag_act")
        s_diag = sem("s_diag")
        s_dT_ps = sem("s_dT_ps")
        s_dT = sem("s_dT")
        s_w2t_ps = sem("s_w2t_ps")
        s_w2t = sem("s_w2t")
        s_F_ps = sem("s_F_ps")
        s_F = sem("s_F")
        s_w12_ps = sem("s_w12_ps")
        s_w12 = sem("s_w12")
        s_T_ps = sem("s_T_ps")
        s_T = sem("s_T")
        s_z2_ps = sem("s_z2_ps")
        s_z1_ps = sem("s_z1_ps")
        s_z2 = sem("s_z2")
        s_z1 = sem("s_z1")
        s_h1_ps = sem("s_h1_ps")
        s_h1 = sem("s_h1")
        s_h2_ps = sem("s_h2_ps")
        s_h2 = sem("s_h2")
        s_y_ps = sem("s_y_ps")
        s_y = sem("s_y")
        s_out = sem("s_out")

        GROUP_ENDS = [0, N_Z1 + N_OWN, N_Z1 + N_OWN + 8, N_Z1 + PER_CHUNK, N_SLOTS]
        GROUP_READY = [1, 2, 2, 3]
        W12_BATCHES = [[range(n, min(n + 4, end)) for n in range(first, end, 4)]
                       for first, end in zip(GROUP_ENDS, GROUP_ENDS[1:])]
        BATCH_0 = [sum(len(g) for g in W12_BATCHES[:n]) for n in range(len(GROUP_READY))]
        N_BATCHES = BATCH_0[-1] + len(W12_BATCHES[-1])
        W12_BANK = [turn_ps[n % len(turn_ps)] for n in range(BATCH_0[-1])] + \
                   [ring[n % RING] for n in range(N_BATCHES - BATCH_0[-1])]
        TURN_AT = [GROUPS + 2, GROUPS + 5]
        W2_BATCHES = [range(n, min(n + 4, NF)) for n in range(0, NF, 4)]
        NTOP = 7

        block = ctx.enter_context(nc.Block())

        def pack(engine, copy, b, c):
            own_l, cross_l = HALF * c, HALF * (1 - c)
            engine.wait_ge(s_T, NG * b + GROUPS * (c + 1))
            if c == 1:
                alone = T[1][ALONE:ALONE + HALF, HALF:NF, :]
                for q in range(QUARTERS):
                    copy(across[q * ROWS:q * ROWS + HALF, :, :], alone[:, q * N_CROSS:(q + 1) * N_CROSS, :])
                copy(T[0][ALONE:ALONE + HALF, NF, :], alone[:, HALF - 1, :]).then_inc(s_packed, 1)
            copy(T[c][ALONE:ALONE + tri(SHORT), cross_l:cross_l + SHORT, :],
                 T[c][0:tri(SHORT), own_l:own_l + SHORT, :]).then_inc(s_packed, 1)
            if c == 1:
                engine.wait_ge(s_packed, PACKS * b + 3)
            for l, first, end, slot, row in MOVES:
                last = copy(T[c][row:row + end - first, l_of(c, slot), :], T[c][first:end, own_l + l, :])
            last.then_inc(s_packed, 1)

        @block.sync
        def _(sp):
            sp.dma_start(idx[:, 0, :], ids[0:P, :]).then_inc(s_ids, 16)
            sp.dma_start(room_w[0:P // 2, 0:H * NF], W2.rearrange("h i l -> h (i l)")[0:P // 2, :]).then_inc(s_w2, 16)
            sp.dma_start(w1_nat[:, :, :], W1).then_inc(s_w1, 16)
            sp.dma_start(idx[:, 1:BLOCKS, :],
                         ids[P:BATCH, :].rearrange("(q p) f -> p q f", p=P)).then_inc(s_more_ids, 16)
            sp.dma_start(w1f[:, FW - 1:FW], b1.rearrange("(p o) -> p o", o=1)).then_inc(s_w1, 16)
            sp.dma_start(dense_nat[:, :, 0:ND], dense.rearrange("(q p) d -> p q d", p=P)).then_inc(s_dense, 16)
            sp.wait_ge(s_F_ps, 1)
            sp.dma_start(top1[:, :, :], W_top1[0:2 * P, :].rearrange("(c p) n -> p c n", p=P)).then_inc(s_top, 16)
            sp.dma_start(top1d[0:ND, :], W_top1[2 * P:2 * P + ND, :]).then_inc(s_top, 16)
            sp.dma_start(top1d[ND:ND + 1, :], b_top1.rearrange("(o n) -> o n", o=1)).then_inc(s_top, 16)
            sp.dma_start(top2[:, :, :], W_top2.rearrange("(c p) n -> p c n", p=P)).then_inc(s_top, 16)
            sp.dma_start(b2_sb[:, :], b2.rearrange("(p o) -> p o", o=1)).then_inc(s_top, 16)
            with nc.allow_non_contiguous_dma(reason="a few hundred words"):
                sp.dma_start(bt2[:, :], b_top2.rearrange("(c p) -> p c", p=P)).then_inc(s_top, 16)
                sp.dma_start(top3[:, :], W_top3.rearrange("(c p) o -> p (c o)", p=P)).then_inc(s_top, 16)
            with nc.sync.Fori(0, BLOCKS) as b:
                sp.wait_ge(s_y, b + 1)
                sp.dma_start(out[bass.ds(b * P, P), :].rearrange("p o -> o p"), y[:, :]).then_inc(s_out, 16)
            sp.wait_ge(s_out, 16 * BLOCKS)

        @block.gpsimd
        def _(pool):
            nc.gpsimd.memset(ident[:, :], 0.0).then_inc(s_ident0, 1)
            pool.wait_ge(s_ident0, 1)
            nc.gpsimd.affine_select(out=ident[:, :], in_=ident[:, :], compare_op=ALU.not_equal, fill=1.0, base=0,
                                    pattern=[[-1, P]], channel_multiplier=1).then_inc(s_ident, 1)

            def gather(f, rows):
                nc.gpsimd.indirect_dma_start(emb[:, f, :], None, tables[f],
                                             bass.IndirectOffsetOnAxis(ap=rows, axis=0)).then_inc(s_emb[f], 16)

            def gathers(b):
                for part in range(len(PARTS) - 1):
                    pool.wait_ge(s_idx, (b - 1) * (len(PARTS) - 1) + part + 1)
                    pool.sem_inc(s_room, 1)
                    for f in range(PARTS[part], PARTS[part + 1]):
                        gather(f, idx_now[:, f:f + 1])

            pool.wait_ge(s_ids, 16)
            for f in range(NF):
                gather(f, idx[:, 0, f:f + 1])
            with nc.gpsimd.Fori(1, BLOCKS) as b:
                gathers(b)

        @block.scalar
        def _(act):
            act.dma_start(room_w[P // 2:P, 0:H * NF], W2.rearrange("h i l -> h (i l)")[P // 2:P, :]).then_inc(s_w2, 16)
            act.wait_ge(s_set, 1)
            nc.scalar.copy(diag[:, :, :, :].rearrange("p r l q -> p (r l q)"),
                           zero[:, 0:1].to_broadcast([P, ROWS * NL * QUARTERS])).then_inc(s_clear, 1)
            nc.scalar.copy(w12t[:, :, :].rearrange("p s n -> p (s n)"),
                           zero[:, 0:1].to_broadcast([P, N_SLOTS * P])).then_inc(s_clear, 1)
            act.wait_ge(s_clear, 1)
            for q in range(QUARTERS):
                last = nc.scalar.copy(diag[q * ROWS:(q + 1) * ROWS, :, NF, q],
                                      one[q * ROWS:(q + 1) * ROWS, 0:1].to_broadcast([ROWS, ROWS]))
            last.then_inc(s_clear, 1)
            act.wait_ge(s_dT_ps, 1)
            dense_ps = h1_ps[0][0:ND + 1, :].rearrange("p (b q r) -> p b q r", b=BLOCKS, q=QUARTERS)
            nc.scalar.copy(denseT[:, :, :].rearrange("p b (r q) -> p b q r", q=QUARTERS), dense_ps).then_inc(s_dT, 1)

            def keep_w2t(n):
                batch = W2_BATCHES[n]
                act.wait_ge(s_w2t_ps, n + 1)
                nc.scalar.copy(w2t[:, batch[0]:batch[-1] + 1, :], turn_ps[n % 2][:, 0:len(batch) * P].rearrange(
                    "p (l h) -> p l h", h=P)).then_inc(s_w2t, 1)

            def spread(b, part, quarters=range(QUARTERS)):
                f0, f1 = CUTS[b][part], CUTS[b][part + 1]
                for q in quarters:
                    quarter = slice(q * ROWS, (q + 1) * ROWS)
                    if q == 0:
                        act.wait_ge(s_turned, NF * b + f1)
                    last = nc.scalar.copy(diag[quarter, :, f0:f1, q], embT[quarter, :, f0:f1])
                    if q == QUARTERS - 1:
                        last.then_inc(s_diag_act, 1)

            keep_w2t(0)
            keep_w2t(1)
            for c in range(NF):
                act.wait_ge(s_F_ps, c + 1)
                nc.scalar.copy(F[:, c, :], ring[c % RING][:, 0:FW]).then_inc(s_F, 1)
                if c % 4 == 3 and c // 4 + 2 < len(W2_BATCHES):
                    keep_w2t(c // 4 + 2)
                if c in SPREAD_AT:
                    part, q = divmod(SPREAD_AT.index(c), QUARTERS)
                    spread(0, part, [q])
            for part in range(len(SPREAD_AT) // QUARTERS, NCUT[0]):
                spread(0, part)

            def keep_T(b, first, end):
                for n in range(first, end):
                    c, g = divmod(n, GROUPS)
                    act.wait_ge(s_T_ps, NG * b + n + 1)
                    rows = ROWS_OF[c]
                    src = ring[n % RING][0:rows, 0:PER * WIDE].rearrange("p (r l q) -> p l r q", r=PER, q=QUARTERS)
                    dst = T[c][0:rows, :, g * PER * QUARTERS:(g + 1) * PER * QUARTERS].rearrange(
                        "p l (r q) -> p l r q", q=QUARTERS)
                    nc.scalar.copy(dst, src).then_inc(s_T, 1)

            def keep_z1(b):
                act.wait_ge(s_z1_ps, b + 1)
                nc.scalar.copy(z[:, 0, :], z1_ps[:, 0:P]).then_inc(s_z1, 1)

            def keep_z2(b):
                act.wait_ge(s_z2_ps, b + 1)
                nc.scalar.activation(z[:, 1, :], z2_ps[:, 0:P], ACT.Identity, bias=kb2[:, 0:1]).then_inc(s_z2, 1)

            def relu1(b):
                for half in range(2):
                    act.wait_ge(s_h1_ps, 2 * b + half + 1)
                    nc.scalar.activation(h1[:, half * M1H:(half + 1) * M1H, :], h1_ps[half][:, 0:M1H * P].rearrange(
                        "p (m n) -> p m n", n=P), ACT.Relu).then_inc(s_h1, 1)

            def relu2(b):
                for m in range(M2):
                    act.wait_ge(s_h2_ps, M2 * b + m + 1)
                    nc.scalar.activation(h2[:, m, :], h2_at[m], ACT.Relu,
                                         bias=bt2[:, m:m + 1]).then_inc(s_h2, 1)

            def keep_y(b, later=True):
                act.wait_ge(s_y_ps, b + 1)
                if later:
                    act.wait_ge(s_out, 16 * b)
                nc.scalar.copy(y[:, :].rearrange("p (q r) -> p r q", q=QUARTERS),
                               y_ps.rearrange("p (r q) -> p r q", q=QUARTERS)).then_inc(s_y, 1)

            def keep_w12(group):
                for n, slots in enumerate(W12_BATCHES[group], BATCH_0[group]):
                    act.wait_ge(s_w12_ps, n + 1)
                    nc.scalar.copy(w12[:, slots[0]:slots[-1] + 1, :], W12_BANK[n][:, 0:len(slots) * P].rearrange(
                        "p (s h) -> p s h", h=P)).then_inc(s_w12, 1)

            keep_w12(0)
            keep_T(0, 0, TURN_AT[0])
            keep_w12(1)
            keep_T(0, TURN_AT[0], TURN_AT[1])
            keep_w12(2)
            pack(act, nc.scalar.copy, 0, 0)
            keep_T(0, TURN_AT[1], NG)
            act.wait_ge(s_top, 16 * NTOP)
            nc.scalar.mul(kb2[:, :], b2_sb[:, :], float(K)).then_inc(s_kb2, 1)
            pack(act, nc.scalar.copy, 0, 1)
            keep_w12(3)
            act.wait_ge(s_kb2, 1)
            spread(1, 0)
            spread(1, 1)
            keep_z1(0)
            spread(1, 2)
            keep_z2(0)
            relu1(0)
            spread(1, 3)
            relu2(0)

            def block_after(b, later=True):
                keep_y(b - 1, later)
                keep_T(b, 0, NG)
                keep_z1(b)
                keep_z2(b)
                relu1(b)
                relu2(b)

            block_after(1, False)
            with nc.scalar.Fori(2, BLOCKS) as b:
                block_after(b)
            keep_y(BLOCKS - 1)

        @block.vector
        def _(dve):
            nc.vector.memset(zero[:, :], 0.0)
            nc.vector.memset(one[:, :], 1.0).then_inc(s_set, 1)
            nc.vector.memset(own_w[:, 0:SHORT, 0:tri(SHORT)], 0.0)
            nc.vector.memset(dense_nat[:, :, ND:ND + 1], 1.0)
            nc.vector.memset(idx[:, BLOCKS, :], 0)
            nc.vector.memset(across[:, :, :], 0.0)
            for c in range(NCH):
                nc.vector.memset(pairs[c][:, :, NP:NP + 1], 1.0)
                last = nc.vector.memset(pairs[c][:, :, NP + 1:ALONE], 0.0)
            last.then_inc(s_set, 1)
            dve.wait_ge(s_more_ids, 16)

            def turn(b, f):
                dve.wait_ge(s_emb[f], 16 * (b + 1))
                nc.vector.transpose(embT[:, :, f], emb[:, f, :]).then_inc(s_turned, 1)
                if f + 1 in PARTS:
                    fields = slice(PARTS[PARTS.index(f + 1) - 1], f + 1)
                    ids_next = idx[:, bass.ds(b + 1, 1), fields].rearrange("p o f -> p (o f)")
                    nc.vector.tensor_copy(idx_now[:, fields], ids_next).then_inc(s_idx, 1)

            def multiply(b, f):
                c, j = divmod(f, HALF)
                f0 = HALF * c
                dve.wait_ge(s_turned, NF * b + f + 1)
                last = nc.vector.tensor_tensor(pairs[c][:, :, tri(j):tri(j + 1)], embT[:, :, f0:f + 1],
                                               embT[:, :, f:f + 1].to_broadcast([P, ROWS, j + 1]), ALU.mult)
                if j == HALF - 1:
                    last.then_inc(s_pairs, 1)

            def add_alone():
                nc.vector.tensor_copy(pairs[1][:, :, ALONE:ALONE + HALF], embT[:, :, 0:HALF])

            def spread(b, f0, f1):
                dve.wait_ge(s_turned, NF * b + f1)
                for q in range(QUARTERS):
                    quarter = slice(q * ROWS, (q + 1) * ROWS)
                    last = nc.vector.tensor_copy(diag[quarter, :, f0:f1, q], embT[quarter, :, f0:f1])
                return last

            def products(b, c, first=0, end=HALF):
                for j in range(first, end + (end == HALF)):
                    f = HALF * c + j
                    if j < HALF:
                        turn(b, f)
                    if j == 0 and c == 1:
                        add_alone()
                    elif j > 0:
                        multiply(b, f - 1)

            def start_block(b):
                dve.wait_ge(s_pairs, NCH * b)

            def start_pairs(b, c):
                dve.wait_ge(s_T_ps, NG * b - NG + GROUPS * (c + 1))

            def work_on(b):
                start_block(b)
                for f in range(NF + 1):
                    if f == NF - 1:
                        dve.wait_ge(s_emb[f], 16 * (b + 1))
                        for q in range(QUARTERS):
                            quarter = slice(q * ROWS, (q + 1) * ROWS)
                            last = nc.vector.transpose(diag[quarter, :, f, q], emb[quarter, f, :])
                        last.then_inc(s_diag, 1)
                    if f < NF:
                        turn(b, f)
                    if f == 0:
                        start_pairs(b, 0)
                    if f + 1 in SPREAD_TO:
                        n = SPREAD_TO.index(f + 1)
                        if n == 0:
                            dve.wait_ge(s_T_ps, NG * b)
                        spread(b, SPREAD_TO[n - 1] if n else 0, f + 1)
                    if f > 0:
                        multiply(b, f - 1)
                    if f == HALF:
                        start_pairs(b, 1)
                        add_alone()
                    if f in PACK_AT:
                        pack(dve, nc.vector.tensor_copy, b - 1, PACK_AT.index(f))

            def F_own(c, w, a, b):
                w = slice(HALF * c + w.start, HALF * c + w.stop) if isinstance(w, slice) else HALF * c + w
                if c == 0:
                    return same[:, w, a, b]
                return same[:, w, b, slice(a.start + 1, a.stop + 1) if isinstance(a, slice) else a + 1]

            def join_own(c, step, first=0, end=HALF):
                swap = "p i l -> p l i"
                for j in range(first, end):
                    pairs_j = slice(tri(j), tri(j) + j + 1)
                    if step == 0:
                        last = nc.vector.tensor_copy(own_w[:, j, pairs_j], F_own(c, j, j, slice(0, j + 1)))
                        if j + 1 < HALF:
                            second = F_own(c, j, slice(j + 1, HALF), slice(0, j + 1))
                            last = nc.vector.tensor_tensor(own_w[:, j + 1:HALF, pairs_j],
                                                           F_own(c, slice(j + 1, HALF), j, slice(0, j + 1)),
                                                           second if c == 0 else second.rearrange(swap), ALU.add)
                    elif step == 1 and j > 0:
                        rows = own_w[:, j:HALF, tri(j):tri(j) + j]
                        third = F_own(c, slice(0, j), slice(j, HALF), j)
                        last = nc.vector.tensor_tensor(rows, rows, third.rearrange(swap), ALU.add)
                if step == 2:
                    slots = slice(slot_of(c, N_OWN), slot_of(c, N_OWN + SHORT))
                    nc.vector.tensor_copy(w12t[:, slots, ALONE:ALONE + tri(SHORT)], own_w[:, 0:SHORT, 0:tri(SHORT)])
                    for l, p0, p1, slot, row in MOVES:
                        nc.vector.tensor_copy(w12t[:, slot_of(c, slot), row:row + p1 - p0], own_w[:, l, p0:p1])
                    for s, l in enumerate(OWN):
                        last = nc.vector.tensor_copy(w12t[:, slot_of(c, s), 0:tri(l + 1)], own_w[:, l, 0:tri(l + 1)])
                return last

            def join_cross(c, step):
                swap = "p i l -> p l i"
                for j in range(HALF):
                    rows = w12t[:, slot_of(c, N_OWN):slot_of(c, PER_CHUNK), tri(j):tri(j) + j + 1]
                    if step == 0 and c == 0:
                        last = nc.vector.tensor_tensor(rows, same[:, HALF:NF, j, 0:j + 1], mixed[:, j, :, 0:j + 1],
                                                       ALU.add)
                    elif step == 0:
                        last = nc.vector.tensor_tensor(rows, same[:, 0:HALF, 0:j + 1, j + 1],
                                                       mixed[:, HALF + j, 0:j + 1, :].rearrange(swap), ALU.add)
                    elif j > 0:
                        third = mixed[:, 0:j, :, j] if c == 0 else mixed[:, HALF:HALF + j, j, :]
                        rows = rows[:, :, 0:j]
                        last = nc.vector.tensor_tensor(rows, rows, third.rearrange(swap), ALU.add)
                if step == 0:
                    other = slice(HALF * (1 - c), HALF * (2 - c))
                    last = nc.vector.tensor_copy(w12t[:, slot_of(c, N_OWN):slot_of(c, PER_CHUNK), NP:NP + 1],
                                                 F[:, other, FW - 1:FW])
                return last

            products(0, 0, 0, FIRST)

            dve.wait_ge(s_w1, 32)
            w1_same = w1f[:, 0:SAME].rearrange("p (r s) -> p r s", s=HALF + 1)
            w1_mixed = w1f[:, SAME:FW - 1].rearrange("p (b a) -> p b a", a=HALF)
            turned = w1_nat[:, :, :].rearrange("p a b -> p b a")
            flat = w1_nat[:, :, :].rearrange("p a b -> p (a b)")
            nc.vector.tensor_tensor(w1_mixed, w1_nat[:, HALF:NF, 0:HALF], turned[:, HALF:NF, 0:HALF], ALU.add)
            nc.vector.tensor_tensor(w1_same[:, :, 0:HALF], w1_nat[:, 0:HALF, 0:HALF], turned[:, 0:HALF, 0:HALF],
                                    ALU.add).then_inc(s_w1f0, 1)
            dve.wait_ge(s_w1f0, 1)
            for r in range(HALF):
                b_r = HALF + r
                last = nc.vector.tensor_tensor(w1_same[:, r, r + 1:HALF + 1], w1_nat[:, b_r, b_r:NF],
                                               turned[:, b_r, b_r:NF], ALU.add)
            last.then_inc(s_w1f0, 1)
            dve.wait_ge(s_w1f0, 2)
            nc.vector.tensor_copy(w1f[:, 0:SAME:HALF + 2], flat[:, 0:HALF * (NF + 1) - NF:NF + 1])
            nc.vector.tensor_copy(w1f[:, 1:SAME:HALF + 2], flat[:, HALF * (NF + 1):NF * NF:NF + 1]).then_inc(s_w1f, 1)

            products(0, 0, FIRST, SECOND)

            dve.wait_ge(s_w1f, 1)
            dve.wait_ge(s_clear, 2)
            for j in range(HALF):
                nc.vector.tensor_copy(w12t[:, 0, tri(j):tri(j + 1)], w1_same[:, j, 0:j + 1])
                nc.vector.tensor_copy(w12t[:, 1, tri(j):tri(j + 1)], w1_same[:, 0:j + 1, j + 1])
            nc.vector.tensor_copy(w12t[:, 0, NP:NP + 1], w1f[:, FW - 1:FW])
            nc.vector.tensor_copy(w12t[:, 0, ALONE:ALONE + HALF], w1_mixed[:, HALF - 1, :])
            for q in range(QUARTERS):
                nc.vector.tensor_copy(w12t[:, NCH:N_Z1, q * ROWS:q * ROWS + HALF],
                                      w1_mixed[:, q * N_CROSS:(q + 1) * N_CROSS, :])

            products(0, 0, SECOND)
            products(0, 1, 0, EARLY)
            dve.wait_ge(s_clear, 1)
            spread(0, 0, HALF).then_inc(s_diag, 1)
            dve.wait_ge(s_F, HALF)
            f = HALF + EARLY
            for n, (step, first, end) in enumerate(JOIN_A):
                turn(0, f)
                f += 1
                if n > 0:
                    dve.wait_ge(s_fold, n)
                join_own(0, step, first, end).then_inc(s_fold if step < 2 else s_w12t, 1)
            waiting = list(range(HALF + EARLY - 1, NF))
            for f in range(f, NF):
                turn(0, f)
                for f1 in waiting[:LATE]:
                    multiply(0, f1)
                waiting = waiting[LATE:]
            for f1 in waiting:
                multiply(0, f1)

            dve.wait_ge(s_F, NF)
            join_cross(0, 0).then_inc(s_fold, 1)
            dve.wait_ge(s_fold, len(JOIN_A))
            join_cross(0, 1).then_inc(s_w12t, 1)
            dve.wait_ge(s_w12t, 1)
            join_own(1, 0).then_inc(s_fold, 1)
            join_cross(1, 0).then_inc(s_fold, 1)
            dve.wait_ge(s_fold, len(JOIN_A) + 1)
            join_own(1, 1).then_inc(s_fold, 1)
            dve.wait_ge(s_fold, len(JOIN_A) + 2)
            join_cross(1, 1)
            dve.wait_ge(s_fold, len(JOIN_A) + 3)
            join_own(1, 2).then_inc(s_w12t, 1)
            start_block(1)
            dve.wait_ge(s_diag_act, NCUT[0])
            start_pairs(1, 0)
            for turned, multiplied in BLOCK_1:
                for f in turned:
                    turn(1, f)
                for f in multiplied:
                    multiply(1, f)
            start_pairs(1, 1)
            add_alone()
            for f in range(HALF, NF):
                multiply(1, f)
            dve.wait_ge(s_diag_act, sum(NCUT))
            with nc.vector.Fori(2, BLOCKS) as b:
                work_on(b)
            pack(dve, nc.vector.tensor_copy, BLOCKS - 1, 0)
            pack(dve, nc.vector.tensor_copy, BLOCKS - 1, 1)

        @block.tensor
        def _(pe):
            pe.wait_ge(s_ident, 1)
            pe.wait_ge(s_dense, 16)
            pe.wait_ge(s_set, 2)
            for b in range(BLOCKS):
                last = nc.tensor.transpose(h1_ps[0][0:ND + 1, b * P:(b + 1) * P], dense_nat[:, b, :], ident[:, :])
            last.then_inc(s_dT_ps, 1)
            pe.wait_ge(s_w2, 32)

            def turn_w2(n):
                batch = W2_BATCHES[n]
                if n >= 2:
                    pe.wait_ge(s_w2t, n - 1)
                for l in batch:
                    last = nc.tensor.transpose(turn_ps[n % 2][:, (l - batch[0]) * P:(l - batch[0] + 1) * P],
                                               w2_nat[:, :, l], ident[:, :])
                last.then_inc(s_w2t_ps, 1)

            turn_w2(0)
            turn_w2(1)
            pe.wait_ge(s_w1f, 1)
            for c in range(NF):
                pe.wait_ge(s_w2t, c // 4 + 1)
                if c >= RING:
                    pe.wait_ge(s_F, c - RING + 1)
                nc.tensor.matmul(ring[c % RING][:, 0:FW], w2t[:, c, :], w1f[:, :],
                                 start=True, stop=True).then_inc(s_F_ps, 1)
                if c % 4 == 1 and c // 4 + 2 < len(W2_BATCHES):
                    turn_w2(c // 4 + 2)

            def sums(b, first, end, fresh=False):
                for n in range(first, end):
                    c, g = divmod(n, GROUPS)
                    if n == first:
                        pe.wait_ge(s_pairs, NCH * b + c + 1)
                    if not fresh or n >= RING:
                        pe.wait_ge(s_T, NG * b + n - RING + 1)
                    for i in range(PER):
                        r = g * PER + i
                        last = nc.tensor.matmul(ring[n % RING][0:ROWS_OF[c], i * WIDE:(i + 1) * WIDE],
                                                pairs[c][:, r, :], diag[:, r, :, :], start=True, stop=True)
                    last.then_inc(s_T_ps, 1)

            def turn_w12(group):
                pe.wait_ge(s_w12t, GROUP_READY[group])
                for n, slots in enumerate(W12_BATCHES[group], BATCH_0[group]):
                    if n in range(len(turn_ps), BATCH_0[-1]):
                        pe.wait_ge(s_w12, n + 1 - len(turn_ps))
                    elif n - RING in range(BATCH_0[-1], N_BATCHES):
                        pe.wait_ge(s_w12, n + 1 - RING)
                    for i, slot in enumerate(slots):
                        last = nc.tensor.transpose(W12_BANK[n][:, i * P:(i + 1) * P], w12t[:, slot, :], ident[:, :])
                    last.then_inc(s_w12_ps, 1)

            def add_z2(c, slots, first=False, last=False):
                for i, s in enumerate(slots):
                    rows = slice(0, rows_of(s))
                    done = nc.tensor.matmul(z2_ps[:, 0:P], w12[rows, slot_of(c, s), :], T[c][rows, l_of(c, s), :],
                                            start=(first and i == 0), stop=(last and i == len(slots) - 1))
                return done

            def weigh_chunk0(b):
                pe.wait_ge(s_T, NG * b + GROUPS)
                add_z2(0, STAY, first=True)
                pe.wait_ge(s_packed, PACKS * b + 2)
                add_z2(0, MOVE)

            def weigh_z1(b):
                pe.wait_ge(s_packed, PACKS * b + 3)
                o = z1_ps[:, 0:P]
                k = ALONE + HALF
                nc.tensor.matmul(o, w12[0:k, 0, :], T[0][0:k, NF, :], start=True, stop=False)
                nc.tensor.matmul(o, w12[0:NP, 1, :], T[1][0:NP, NF, :], start=False, stop=False)
                for i in range(N_CROSS):
                    last = nc.tensor.matmul(o, w12[0:k, NCH + i, :], across[0:k, i, :], start=False,
                                            stop=(i == N_CROSS - 1))
                last.then_inc(s_z1_ps, 1)

            def weigh_chunk1(b):
                pe.wait_ge(s_T, NG * b + NG)
                add_z2(1, STAY)
                pe.wait_ge(s_packed, PACKS * (b + 1))
                add_z2(1, MOVE, last=True).then_inc(s_z2_ps, 1)

            def h1_at(m):
                return h1_ps[m // M1H][:, m % M1H * P:(m % M1H + 1) * P]

            def layer1_dense(dense_block):
                for m in range(M1):
                    nc.tensor.matmul(h1_at(m), top1d[:, m * P:(m + 1) * P], dense_block, start=(m % M1H == 0),
                                     stop=False)

            def layer1(b):
                for half in range(2):
                    for part, ready in ((0, s_z1), (1, s_z2)):
                        if half == 0:
                            pe.wait_ge(ready, b + 1)
                        for m in range(half * M1H, (half + 1) * M1H):
                            last = nc.tensor.matmul(h1_at(m), top1[:, part, m * P:(m + 1) * P], z[:, part, :],
                                                    start=False, stop=(part == 1 and m % M1H == M1H - 1))
                    last.then_inc(s_h1_ps, 1)

            def layer2(b):
                for half in range(2):
                    pe.wait_ge(s_h1, 2 * b + half + 1)
                    for m in range(M2):
                        for c in range(half * M1H, (half + 1) * M1H):
                            last = nc.tensor.matmul(h2_at[m], top2[:, c, m * P:(m + 1) * P], h1[:, c, :],
                                                    start=(c == 0), stop=(c == M1 - 1))
                        if half == 1:
                            last.then_inc(s_h2_ps, 1)

            def layer3(b):
                for m in range(M2):
                    pe.wait_ge(s_h2, M2 * b + m + 1)
                    last = nc.tensor.matmul(y_ps, top3[:, m:m + 1], h2[:, m, :], start=(m == 0), stop=(m == M2 - 1))
                last.then_inc(s_y_ps, 1)

            pe.wait_ge(s_dT, 1)
            pe.wait_ge(s_w2t, len(W2_BATCHES))
            turn_w12(0)
            pe.wait_ge(s_F, NF)
            pe.wait_ge(s_clear, 3)
            pe.wait_ge(s_top, 16 * NTOP)
            layer1_dense(denseT[:, 0, :])
            pe.wait_ge(s_diag, 1)
            pe.wait_ge(s_diag_act, NCUT[0])
            sums(0, 0, GROUPS, True)
            sums(0, GROUPS, TURN_AT[0])
            turn_w12(1)
            sums(0, TURN_AT[0], TURN_AT[1])
            turn_w12(2)
            sums(0, TURN_AT[1], NG)
            pe.wait_ge(s_w12, BATCH_0[-1])
            weigh_chunk0(0)
            pe.wait_ge(s_T, NG)
            turn_w12(3)
            weigh_z1(0)
            pe.wait_ge(s_w12, N_BATCHES)
            weigh_chunk1(0)
            layer1(0)
            layer2(0)

            def block_after(b):
                sums(b, 0, GROUPS)
                sums(b, GROUPS, NG)
                weigh_chunk0(b)
                weigh_z1(b)
                weigh_chunk1(b)
                layer1(b)
                layer2(b)

            layer1_dense(denseT[:, 1, :])
            layer3(0)
            pe.wait_ge(s_diag_act, sum(NCUT))
            block_after(1)
            with nc.tensor.Fori(2, BLOCKS) as b:
                layer1_dense(denseT[:, bass.ds(b, 1), :].rearrange("p o n -> p (o n)"))
                layer3(b - 1)
                pe.wait_ge(s_diag, b)
                block_after(b)
            layer3(BLOCKS - 1)


def kernel(**inputs):
    import numpy as np
    import concourse.bacc as bacc
    from concourse.bass_utils import run_bass_kernel_spmd as run

    nc = bacc.Bacc("TRN2", target_bir_lowering=False, num_devices=1)
    arrays, aps = {}, {}
    for name, value in inputs.items():
        a = np.ascontiguousarray(value)
        arrays[f"in_{name}"] = a
        aps[name] = nc.dram_tensor(f"in_{name}", a.shape, mybir.dt.from_np(a.dtype), kind="ExternalInput").ap()
    batch, fields = aps["ids"].shape
    out = nc.dram_tensor("out_y", (batch, 1), F32, kind="ExternalOutput").ap()
    dlrm_tower(nc, aps["dense_ctx"], aps["ids"], [aps[f"tbl_{f}"] for f in range(fields)],
               aps["W_top1"], aps["b_top1"], aps["W_top2"], aps["b_top2"], aps["W_top3"],
               aps["L0_rec_W1"], aps["L0_rec_b1"], aps["L0_rec_W2"], aps["L0_rec_b2"], out)
    return run(nc, [arrays], core_ids=[0]).results[0]["out_y"]
```
